# Optimizing a Trainium2 kernel written in Bass

```python
import numpy as np
import jax
import jax.numpy as jnp

def _softmax(x, axis=-1):
    return jax.nn.softmax(x, axis=axis)

def _gelu(x):
    return jax.nn.gelu(x, approximate=True)

def _silu(x):
    return jax.nn.silu(x)

def _sigmoid(x):
    return jax.nn.sigmoid(x)

def _layernorm(x, axis=-1, eps=1e-05):
    m = jnp.mean(x, axis=axis, keepdims=True)
    v = jnp.var(x, axis=axis, keepdims=True)
    return (x - m) / jnp.sqrt(v + eps)

def _scatter_add(tgt, idx, src, axis=0):
    return tgt.at[idx].add(src)

def _segment_sum(src, seg, n):
    return jax.ops.segment_sum(src, seg, n)
kernel_name = 'mk_perceiver_d1_seqx_r8_22f2fb'

def setup_inputs(seed: int=0):
    np.random.seed(seed)
    _w = jnp.asarray

    def _rec_inputs():
        import jax
        import jax.numpy as jnp
        _rk = jax.random.key(seed)
        x = -0.0002928 + 1 * jax.random.normal(jax.random.fold_in(_rk, 1), (4, 128, 128), jnp.float32)
        _lenS = 128 - jax.random.randint(jax.random.fold_in(_rk, 7), (4,), 0, max(1, 128 // 4) + 1, jnp.int32)
        _lenS2 = 2048 - jax.random.randint(jax.random.fold_in(_rk, 8), (4,), 0, max(1, 2048 // 4) + 1, jnp.int32)
        _ctx_1024P = jax.random.normal(jax.random.fold_in(_rk, 11), (4, 16, 128), jnp.float32)
        _ctx_1024c = jax.random.dirichlet(jax.random.fold_in(_rk, 511), 0.3 * jnp.ones((16,), jnp.float32), (4, 2048))
        _ctx_1024t = jnp.einsum('bsk,bkd->bsd', _ctx_1024c, _ctx_1024P)
        _ctx_1024t = _ctx_1024t * jax.lax.rsqrt(jnp.mean(jnp.square(_ctx_1024t)) + 1e-12) * 0.953939
        ctx_1024 = -1.39393e-06 + 0.999914 * (_ctx_1024t + 0.3 * jax.random.normal(jax.random.fold_in(_rk, 611), (4, 2048, 128), jnp.float32))
        _validS = jnp.arange(128)[None, :] < _lenS[:, None]
        _validS2 = jnp.arange(2048)[None, :] < _lenS2[:, None]
        _causal = jnp.tril(jnp.ones((128, 128), dtype=bool))
        mask_Bx1xSxS2_if1 = jnp.where(jnp.ones((4, 1, 128, 2048), dtype=bool), 1, 0).astype(jnp.int32)
        return (x, ctx_1024, mask_Bx1xSxS2_if1)
    x, ctx_1024, mask_Bx1xSxS2_if1 = _rec_inputs()

    def _L0_xattn_setup():
        import jax, jax.numpy as jnp
        import numpy as np
        D_MODEL = 128
        N_HEADS = 16
        D_K = D_MODEL // N_HEADS
        B, S = (2, 256)
        key = jax.random.key(seed)
        ks = jax.random.split(key, 12)
        sc = 1.0 / np.sqrt(D_MODEL)
        inp = {'q': jax.random.normal(ks[0], (B, S, D_MODEL), jnp.float32), 'k': jax.random.normal(ks[1], (B, S, D_MODEL), jnp.float32), 'v': jax.random.normal(ks[2], (B, S, D_MODEL), jnp.float32), 'mask': jnp.ones((B, 1, S, S), jnp.int32), 'Wq': jax.random.normal(ks[3], (D_MODEL, D_MODEL), jnp.float32) * sc, 'bq': jnp.zeros((D_MODEL,), jnp.float32), 'Wk': jax.random.normal(ks[4], (D_MODEL, D_MODEL), jnp.float32) * sc, 'bk': jnp.zeros((D_MODEL,), jnp.float32), 'Wv': jax.random.normal(ks[5], (D_MODEL, D_MODEL), jnp.float32) * sc, 'bv': jnp.zeros((D_MODEL,), jnp.float32), 'Wo': jax.random.normal(ks[6], (D_MODEL, D_MODEL), jnp.float32) * sc, 'bo': jnp.zeros((D_MODEL,), jnp.float32)}
        return inp
    _L0_xattn_all = _L0_xattn_setup()
    _L0_xattn_in = {k: v for k, v in _L0_xattn_all.items() if k in ('Wq', 'bq', 'Wk', 'bk', 'Wv', 'bv', 'Wo', 'bo')}
    del _L0_xattn_all

    def _L0_attn_setup():
        import jax, jax.numpy as jnp
        import numpy as np
        DIM = 128
        B, S = (4, 512)
        key = jax.random.key(seed)
        ks = jax.random.split(key, 7)
        s = 1.0 / np.sqrt(DIM)
        return {'x': jax.random.normal(ks[0], (B, S, DIM), dtype=jnp.float32), 'wq': jax.random.uniform(ks[1], (DIM, DIM), minval=-s, maxval=s, dtype=jnp.float32), 'bq': jax.random.uniform(ks[2], (DIM,), minval=-s, maxval=s, dtype=jnp.float32), 'wk': jax.random.uniform(ks[3], (DIM, DIM), minval=-s, maxval=s, dtype=jnp.float32), 'bk': jax.random.uniform(ks[4], (DIM,), minval=-s, maxval=s, dtype=jnp.float32), 'wv': jax.random.uniform(ks[5], (DIM, DIM), minval=-s, maxval=s, dtype=jnp.float32), 'bv': jax.random.uniform(ks[6], (DIM,), minval=-s, maxval=s, dtype=jnp.float32)}
    _L0_attn_all = _L0_attn_setup()
    _L0_attn_in = {k: v for k, v in _L0_attn_all.items() if k in ('wq', 'bq', 'wk', 'bk', 'wv', 'bv')}
    del _L0_attn_all

    def _L0_ffn_setup():
        import jax, jax.numpy as jnp
        import numpy as np
        D_MODEL = 128
        EXPANSION = 4
        D_HIDDEN = D_MODEL * EXPANSION
        NUM_STAGES = int(np.log2(D_HIDDEN))

        def butterfly(y, weights, dim):
            lead = y.shape[:-1]
            for stage in range(weights.shape[0]):
                s = 2 ** stage
                nb = dim // (2 * s)
                yr = y.reshape(*lead, nb, 2, s)
                a = yr[..., 0, :]
                b = yr[..., 1, :]
                w = weights[stage].reshape(nb, s, 2, 2)
                na = w[..., 0, 0] * a + w[..., 0, 1] * b
                nb2 = w[..., 1, 0] * a + w[..., 1, 1] * b
                y = jnp.stack([na, nb2], axis=-2).reshape(*lead, dim)
            return y
        key = jax.random.key(seed)
        ks = jax.random.split(key, 6)
        B, S = (4, 256)
        x = jax.random.normal(ks[0], (B, S, D_MODEL), jnp.float32)
        W_exp = jax.random.normal(ks[1], (D_MODEL, D_HIDDEN), jnp.float32) * 0.02
        b_exp = jnp.zeros((D_HIDDEN,), jnp.float32)
        up_weights = jax.random.normal(ks[2], (NUM_STAGES, D_HIDDEN // 2, 2, 2), jnp.float32) * 0.02
        up_bias = jnp.zeros((D_HIDDEN,), jnp.float32)
        down_weights = jax.random.normal(ks[3], (NUM_STAGES, D_HIDDEN // 2, 2, 2), jnp.float32) * 0.02
        W_con = jax.random.normal(ks[4], (D_HIDDEN, D_MODEL), jnp.float32) * 0.02
        b_con = jnp.zeros((D_MODEL,), jnp.float32)
        down_bias = jnp.zeros((D_MODEL,), jnp.float32)
        return dict(x=x, W_exp=W_exp, b_exp=b_exp, up_weights=up_weights, up_bias=up_bias, down_weights=down_weights, W_con=W_con, b_con=b_con, down_bias=down_bias)
    _L0_ffn_all = _L0_ffn_setup()
    _L0_ffn_in = {k: v for k, v in _L0_ffn_all.items() if k in ('W_exp', 'b_exp', 'up_weights', 'up_bias', 'down_weights', 'W_con', 'b_con', 'down_bias')}
    del _L0_ffn_all
    return {'x': x, 'ctx_1024': ctx_1024, 'mask_Bx1xSxS2_if1': mask_Bx1xSxS2_if1, 'L0_xattn_Wq': _L0_xattn_in['Wq'], 'L0_xattn_bq': _L0_xattn_in['bq'], 'L0_xattn_Wk': _L0_xattn_in['Wk'], 'L0_xattn_bk': _L0_xattn_in['bk'], 'L0_xattn_Wv': _L0_xattn_in['Wv'], 'L0_xattn_bv': _L0_xattn_in['bv'], 'L0_xattn_Wo': _L0_xattn_in['Wo'], 'L0_xattn_bo': _L0_xattn_in['bo'], 'L0_attn_wq': _L0_attn_in['wq'], 'L0_attn_bq': _L0_attn_in['bq'], 'L0_attn_wk': _L0_attn_in['wk'], 'L0_attn_bk': _L0_attn_in['bk'], 'L0_attn_wv': _L0_attn_in['wv'], 'L0_attn_bv': _L0_attn_in['bv'], 'L0_ffn_W_exp': _L0_ffn_in['W_exp'], 'L0_ffn_b_exp': _L0_ffn_in['b_exp'], 'L0_ffn_up_weights': _L0_ffn_in['up_weights'], 'L0_ffn_up_bias': _L0_ffn_in['up_bias'], 'L0_ffn_down_weights': _L0_ffn_in['down_weights'], 'L0_ffn_W_con': _L0_ffn_in['W_con'], 'L0_ffn_b_con': _L0_ffn_in['b_con'], 'L0_ffn_down_bias': _L0_ffn_in['down_bias']}

def reference(x, ctx_1024, mask_Bx1xSxS2_if1, L0_xattn_Wq, L0_xattn_bq, L0_xattn_Wk, L0_xattn_bk, L0_xattn_Wv, L0_xattn_bv, L0_xattn_Wo, L0_xattn_bo, L0_attn_wq, L0_attn_bq, L0_attn_wk, L0_attn_bk, L0_attn_wv, L0_attn_bv, L0_ffn_W_exp, L0_ffn_b_exp, L0_ffn_up_weights, L0_ffn_up_bias, L0_ffn_down_weights, L0_ffn_W_con, L0_ffn_b_con, L0_ffn_down_bias):
    import jax
    import jax.numpy as jnp

    def _L0_xattn_ref(q, k, v, mask, Wq, bq, Wk, bk, Wv, bv, Wo, bo):
        import jax, jax.numpy as jnp
        import numpy as np
        D_MODEL = 128
        N_HEADS = 16
        D_K = D_MODEL // N_HEADS
        B, S = (2, 256)
        bs = q.shape[0]

        def proj(x, W, b):
            y = x @ W + b
            return y.reshape(bs, -1, N_HEADS, D_K).transpose(0, 2, 1, 3)
        qh, kh, vh = (proj(q, Wq, bq), proj(k, Wk, bk), proj(v, Wv, bv))
        scores = jnp.einsum('bhqd,bhkd->bhqk', qh, kh) / jnp.sqrt(jnp.float32(D_K))
        scores = jnp.where(mask == 0, jnp.float32(-1000000000.0), scores)
        attn = jax.nn.softmax(scores, axis=-1)
        out = jnp.einsum('bhqk,bhkd->bhqd', attn, vh)
        concat = out.transpose(0, 2, 1, 3).reshape(bs, -1, N_HEADS * D_K)
        return concat @ Wo + bo

    def _L0_attn_ref(x, wq, bq, wk, bk, wv, bv):
        import jax, jax.numpy as jnp
        import numpy as np
        DIM = 128
        B, S = (4, 512)
        scale = x.shape[-1] ** (-0.5)
        q = x @ wq.T + bq
        k = x @ wk.T + bk
        v = x @ wv.T + bv
        scores = jnp.einsum('bqd,bkd->bqk', q, k) * scale
        attn = jax.nn.softmax(scores, axis=-1)
        return jnp.einsum('bqk,bkd->bqd', attn, v)

    def _L0_ffn_ref(x, W_exp, b_exp, up_weights, up_bias, down_weights, W_con, b_con, down_bias):
        import jax, jax.numpy as jnp
        import numpy as np
        D_MODEL = 128
        EXPANSION = 4
        D_HIDDEN = D_MODEL * EXPANSION
        NUM_STAGES = int(np.log2(D_HIDDEN))

        def butterfly(y, weights, dim):
            lead = y.shape[:-1]
            for stage in range(weights.shape[0]):
                s = 2 ** stage
                nb = dim // (2 * s)
                yr = y.reshape(*lead, nb, 2, s)
                a = yr[..., 0, :]
                b = yr[..., 1, :]
                w = weights[stage].reshape(nb, s, 2, 2)
                na = w[..., 0, 0] * a + w[..., 0, 1] * b
                nb2 = w[..., 1, 0] * a + w[..., 1, 1] * b
                y = jnp.stack([na, nb2], axis=-2).reshape(*lead, dim)
            return y
        h = jnp.einsum('bsd,dh->bsh', x, W_exp) + b_exp
        h = butterfly(h, up_weights, D_HIDDEN)
        h = jax.nn.gelu(h + up_bias, approximate=False)
        h = butterfly(h, down_weights, D_HIDDEN)
        y = jnp.einsum('bsh,hd->bsd', h, W_con) + b_con
        return y + down_bias
    x = x + _L0_xattn_ref(_layernorm(x, axis=-1), ctx_1024, ctx_1024, mask_Bx1xSxS2_if1, L0_xattn_Wq, L0_xattn_bq, L0_xattn_Wk, L0_xattn_bk, L0_xattn_Wv, L0_xattn_bv, L0_xattn_Wo, L0_xattn_bo)
    x = x + _L0_attn_ref(_layernorm(x, axis=-1), L0_attn_wq, L0_attn_bq, L0_attn_wk, L0_attn_bk, L0_attn_wv, L0_attn_bv)
    x = x + _L0_ffn_ref(_layernorm(x, axis=-1), L0_ffn_W_exp, L0_ffn_b_exp, L0_ffn_up_weights, L0_ffn_up_bias, L0_ffn_down_weights, L0_ffn_W_con, L0_ffn_b_con, L0_ffn_down_bias)
    return x

_drawn_inputs = setup_inputs


def setup_inputs(seed=0):
    import zlib

    import numpy as np

    out = dict(_drawn_inputs(seed))
    spreads = {'L0_xattn_bq': (0.0, 0.333),
     'L0_xattn_bk': (0.0, 0.8),
     'L0_xattn_bv': (0.0, 0.1),
     'L0_xattn_bo': (0.0, 0.1),
     'L0_ffn_b_exp': (0.0, 0.1),
     'L0_ffn_up_bias': (0.0, 0.1),
     'L0_ffn_b_con': (0.0, 0.1),
     'L0_ffn_down_bias': (0.0, 0.1)}
    factors = {'L0_attn_wq': 3.154, 'L0_attn_bq': 8.0, 'L0_attn_wk': 3.066, 'L0_attn_bk': 8.0}
    for name, (base, spread) in spreads.items():
        noise = np.random.default_rng([zlib.crc32(name.encode()), seed]).standard_normal(out[name].shape)
        drawn = base * np.exp(spread * noise) if base else spread * noise
        out[name] = jnp.asarray(drawn.astype(out[name].dtype))
    for name, factor in factors.items():
        out[name] = (out[name] * factor).astype(out[name].dtype)
    return out
```

```python
from contextlib import ExitStack

import concourse.bass as bass
from concourse import mybir

F32 = mybir.dt.float32
BF16 = mybir.dt.bfloat16
I32 = mybir.dt.int32
ALU = mybir.AluOpType
ACT = mybir.ActivationFunctionType
AX = mybir.AxisListType

EPS = 1e-5
Q_PART = (0, 1, 2, 0, 1, 0)
K_PART = (0, 0, 0, 1, 1, 2)
SLOTS = len(Q_PART)


def perceiver_block(nc, x, ctx, mask, w_q, w_k, w_v, w_o, a_wqT, a_wkT, a_wvT, w_exp, b_exp, w_up,
                    up_bias, w_down, w_conT, bias_cols, bias_rows, out, q_scratch, q_full):
    B, S, D = x.shape
    KEYS = ctx.shape[1]
    H, DK = 16, 8
    KT = KEYS // 128
    PAIRS = H // 2
    G = B * PAIRS
    STEPS = KT // 2
    CHUNKS = KEYS // 512
    HID = w_exp.shape[1]
    HB = HID // 128
    STAGES = w_up.shape[0]
    ROWS = 16 * SLOTS
    MROWS = 3
    assert S == 128 and D == 128 and STEPS == 8 and CHUNKS == 4 and HB == 4

    with ExitStack() as es:
        def sb(name, shape, dt=F32):
            return es.enter_context(nc.sbuf_tensor(name, shape, dt))

        def psum(name, shape):
            return es.enter_context(nc.psum_tensor(name, shape, F32))

        def sem(name):
            return es.enter_context(nc.semaphore(name))

        x_sb = sb("x_sb", [128, B, D])
        xo_sb = sb("xo_sb", [128, B, D])
        xn = sb("xn", [128, B, D])
        stats = sb("stats", [128, B, 6])
        moments = sb("moments", [128, B, 2])
        rstd = sb("rstd", [128, B])
        neg_half = sb("neg_half", [128, B])
        xnT = sb("xnT", [128, B * S])
        qf = sb("qf", [128, B * S])
        qrest = sb("qrest", [128, B * S])
        qparts = sb("qparts", [128, 3, B * S], BF16)
        qpair = sb("qpair", [128, 3, B, 2, S], BF16)
        parity = sb("parity", [128, 2])
        ident = sb("ident", [128, 128])
        identb = sb("identb", [128, 128], BF16)
        ones_rows = sb("ones_rows", [MROWS, KEYS // 2])
        cols = sb("cols", [128, 5])
        abq_s = sb("abq_s", [128, 1])
        rows = sb("rows", [128, 4, D])
        out_bias = sb("out_bias", [128, D])
        wq_sb, wk_sb, wv_sb, wo_sb = (sb(n, [128, D]) for n in ("wq_sb", "wk_sb", "wv_sb", "wo_sb"))
        aq_sb, ak_sb, av_sb = (sb(n, [128, D]) for n in ("aq_sb", "ak_sb", "av_sb"))
        ctx_sb = sb("ctx_sb", [128, KT, D])
        ctxT = sb("ctxT", [128, KEYS])
        kparts = sb("kparts", [128, 3, KEYS], BF16)
        krest = sb("krest", [128, 2, 512])
        kstack = sb("kstack", [128, 2, PAIRS, KEYS], BF16)
        qstack = sb("qstack", [128, B, PAIRS, 2 * S], BF16)
        vt = sb("vt", [128, 2, KT, H, DK + 1])
        smax = sb("smax", [128, 2, 2, CHUNKS])
        negmax = sb("negmax", [128, 2, 2])
        mrest = sb("mrest", [128, 2, 2])
        mparts = sb("mparts", [128, 2, 2, MROWS], BF16)
        probs = sb("probs", [128, 4, 512])
        oT = sb("oT", [128, 2, S])
        osum = sb("osum", [128, 2, PAIRS, 2, DK + 1])
        rsum = sb("rsum", [128, 2, PAIRS, 2])
        att = sb("att", [128, D])
        attT = sb("attT", [128, S])
        x1 = sb("x1", [128, D])
        x1v = sb("x1v", [128, D])
        t_stats = sb("t_stats", [128, 6])
        t_mom = sb("t_mom", [128, 2])
        t_rstd = sb("t_rstd", [128, 1])
        t_xn = sb("t_xn", [128, D])
        t_xnT = sb("t_xnT", [128, S])
        s_qT = sb("s_qT", [128, S])
        s_kT = sb("s_kT", [128, S])
        s_v = sb("s_v", [128, D])
        s_negmax = sb("s_negmax", [128, 1])
        s_sum = sb("s_sum", [128, 1])
        s_rsum = sb("s_rsum", [128, 1])
        s_p = sb("s_p", [128, S])
        s_pT = sb("s_pT", [128, S])
        x2 = sb("x2", [128, B, D])
        x2b = sb("x2b", [128, B, D])
        f_xnT = sb("f_xnT", [128, B * S])
        f_h = probs
        stage_w = sb("stage_w", [128, 2, 2 * HID])
        up_y = sb("up_y", [128, 2, HID])
        row_y = sb("row_y", [1, 2, HID])
        down_y = sb("down_y", [128, 2, HID])
        bf_a, bf_b = qf, qrest
        ub_row = sb("ub_row", [1, HID])
        up_b = row_y[:, 0, :]
        up_bcol = sb("up_bcol", [128, HB])
        w_dn = xnT[:].rearrange("p (j d) -> p j d", j=HB)
        y_sb = xn
        mask_min = sb("mask_min", [128, B * CHUNKS])
        mask_low = sb("mask_low", [128, 1])
        flag_f = sb("flag_f", [1, 1])
        flag = sb("flag", [1, 1], I32)
        MRING = 3
        mask_sb = qpair[:].rearrange("p i b h s -> p (i b h s)").bitcast(I32).rearrange("p (r k) -> p r k", r=MRING)
        g_mem = kstack[:].rearrange("p a b k -> p (a b k)").bitcast(F32)
        g_kT, g_keep, g_drop, g_s, g_pT, g_v, g_mask = (g_mem[:, KEYS * i:KEYS * i + KEYS] for i in range(7))
        g_q, g_qh, g_heads, g_negmax, g_sum = (g_mem[:, a:b] for a, b in (
            (14336, 14848), (14848, 14976), (14976, 14992), (14992, 14993), (14993, 14994)))

        ps_a = psum("ps_a", [128, 2, 512])
        ps_b = psum("ps_b", [128, 3, 512])
        ps_o = psum("ps_o", [128, 2, 512])
        ps_m = psum("ps_m", [128, 512])

        in_x, in_x1, in_wq, in_wk, in_wv, in_rows, in_tail = map(sem, ("in_x", "in_x1", "in_wq", "in_wk", "in_wv", "in_rows", "in_tail"))
        in_ctx = [sem(f"in_ctx{c}") for c in range(CHUNKS)]
        in_ffn = sem("in_ffn")
        in_stage = [sem("in_stage0"), sem("in_stage1")]
        q_out0, q_out = sem("q_out0"), sem("q_out")
        q_in = [sem(f"q_in{b}") for b in range(B)]
        k_in = [sem(f"k_in{p}") for p in range(PAIRS)]
        ones_in = sem("ones_in")
        y_out = sem("y_out")
        dve = sem("dve_chain")
        pool = sem("pool_chain")
        act = sem("act_chain")
        consts = sem("consts")
        var_ready, rstd_ready, xn_ready, xnT_ps, xnT_ready, q_ps, qpair_ready = map(
            sem, ("var_ready", "rstd_ready", "xn_ready", "xnT_ps", "xnT_ready", "q_ps", "qpair_ready"))
        ctxT_ps, ctxT_ready, k_ps, k1_ready, k2_ready, k3_ready, v_ps, v_ready = map(
            sem, ("ctxT_ps", "ctxT_ready", "k_ps", "k1_ready", "k2_ready", "k3_ready", "v_ps", "v_ready"))
        a_ps, a_max, b_ps, p_ready, pv_done = map(sem, ("a_ps", "a_max", "b_ps", "p_ready", "pv_done"))
        negmax_ready, mparts_ready, m_ps, m_ready = map(sem, ("negmax_ready", "mparts_ready", "m_ps", "m_ready"))
        oT_ready, o_ps, osum_ready, att_ready, o_clear = map(sem, ("oT_ready", "o_ps", "osum_ready", "att_ready", "o_clear"))
        tail_ps, tail_sb, t_var, t_rs, t_xn_ready, s_max_ready, row_sums = map(
            sem, ("tail_ps", "tail_sb", "t_var", "t_rs", "t_xn_ready", "s_max_ready", "row_sums"))
        up_ready, up_b_ready, down_ready, up_ps, up_bps, up_bcol_ready, gelu_ready, dn_tps, w_dn_ready, dn_ps, y_ready = map(
            sem, ("up_ready", "up_b_ready", "down_ready", "up_ps", "up_bps", "up_bcol_ready", "gelu_ready",
                  "dn_tps", "w_dn_ready", "dn_ps", "y_ready"))

        mask_in = [sem(f"mask_in{r}") for r in range(3)]
        mask_read, low_ready, low_ps, low_read, flag_ready = map(
            sem, ("mask_read", "low_ready", "low_ps", "low_read", "flag_ready"))
        q_saved, g_in_q, g_in_mask, g_mask_read, g_k_ready, g_qh_ready, g_s_ps, g_max_ready, g_p_ready = map(
            sem, ("q_saved", "g_in_q", "g_in_mask", "g_mask_read", "g_k_ready", "g_qh_ready", "g_s_ps", "g_max_ready", "g_p_ready"))
        g_pT_ps, g_pT_ready, g_o_ps, g_o_read, g_dve = map(
            sem, ("g_pT_ps", "g_pT_ready", "g_o_ps", "g_o_read", "g_dve"))

        def chain_of(eng, s):
            n = [0]

            def link(ins, wait=True):
                n[0] += 1
                ins.then_inc(s, 1)
                if wait:
                    eng.wait_ge(s, n[0])
            return link

        LAG = 2
        AHEAD = 2
        PREP = [(what, c) for c in range(CHUNKS) for what in ("turn", "k")] + [("v", c) for c in range(CHUNKS)]
        TAIL = ["turn_att", "project", "turn_x1", "qkv", "scores", "turn_p", "self_out", "turn_x2"]
        TAIL_AT = {(1, 2): 0, (1, 6): 1, (2, 6): 2, (3, 2): 3, (3, 6): 4, (4, 2): 5, (4, 6): 6, (5, 6): 7}

        def misc_task(g, k):
            b, p = divmod(g, PAIRS)
            if k in (0, 4) and b + 1 < B and 2 * p + k // 4 < len(PREP):
                return ("prep", b + 1) + PREP[2 * p + k // 4]
            if b > 0 and (p, k) in TAIL_AT:
                return "tail", b - 1, TAIL[TAIL_AT[p, k]], 0
            if (b, p, k) == (B - 1, 0, 2):
                return "flag", 0, "low", 0
            return None

        def read_of(task):
            kind, b, what, c = task
            if kind == "flag":
                return low_read, 1
            if kind == "prep":
                if what == "k" and b >= B:
                    return g_k_ready, CHUNKS * (b - B) + c + 1
                return {"turn": ctxT_ready, "k": k2_ready, "v": v_ready}[what], CHUNKS * b + c + 1
            return tail_sb, len(TAIL) * b + TAIL.index(what) + 1

        before = {}
        last = (v_ready, CHUNKS)
        for g_ in range(G):
            for k_ in range(STEPS):
                if misc_task(g_, k_):
                    before[misc_task(g_, k_)] = last
                    last = read_of(misc_task(g_, k_))
        for what_ in TAIL:
            before["tail", B - 1, what_, 0] = last
            last = read_of(("tail", B - 1, what_, 0))
        last = (y_ready, B)
        for b_ in range(B, 2 * B):
            for t_ in [("prep", b_) + t for t in PREP] + [("tail", b_, what_, 0) for what_ in TAIL]:
                before[t_] = last
                last = read_of(t_)

        PHASES = ((0, 1), (1, B))
        K_BANK = (ps_a[:, 0, :], ps_a[:, 1, :], ps_o[:, 1, :], ps_b[:, 1, :])
        V_BANK = (ps_m[:], ps_b[:, 0, :], ps_b[:, 2, :], ps_m[:])

        def g_bank(c):
            return ps_a[:, c, :] if c < 2 else ps_b[:, c - 2, :]

        def masked(eng):
            eng.wait_ge(flag_ready, 1)
            return eng.If(eng.value_load(flag[:], min_val=0, max_val=1) == 1)

        block = es.enter_context(nc.Block())

        @block.sync
        def _(sp):
            sp.dma_start(x_sb[:, 0, :], x[0]).then_inc(in_x, 16)
            sp.dma_start(ctx_sb[:, 0:4, :], ctx[0, 0:512, :].rearrange("(t k) d -> k t d", k=128)).then_inc(in_ctx[0], 16)
            sp.dma_start(wq_sb[:], w_q).then_inc(in_wq, 16)
            sp.dma_start(wk_sb[:], w_k).then_inc(in_wk, 16)
            sp.dma_start(cols[:], bias_cols).then_inc(in_wk, 16)
            for c in range(1, CHUNKS):
                sp.dma_start(ctx_sb[:, 4 * c:4 * c + 4, :],
                             ctx[0, 512 * c:512 * c + 512, :].rearrange("(t k) d -> k t d", k=128)).then_inc(in_ctx[c], 16)
                if c == 1:
                    sp.dma_start(x_sb[:, 1:B, :], x[1:B].rearrange("b s d -> s b d")).then_inc(in_x1, 16)
            sp.dma_start(wv_sb[:], w_v).then_inc(in_wv, 16)
            sp.wait_ge(consts, 3)
            for buf in range(2):
                sp.dma_start(kstack[ROWS:ROWS + MROWS, buf, :, :].bitcast(F32),
                             ones_rows[:].unsqueeze(1).broadcast_to([MROWS, PAIRS, KEYS // 2])).then_inc(ones_in, 16)

            def load_q(b):
                for s in range(SLOTS):
                    sp.dma_start(qstack[16 * s:16 * s + 16, b, :, :],
                                 q_scratch[:, Q_PART[s], b, :].rearrange("(p r) c -> r p c", r=16)).then_inc(q_in[b], 16)

            def load_k(b, p, slots=range(SLOTS)):
                for s in slots:
                    sp.dma_start(kstack[16 * s:16 * s + 16, b % 2, p, :],
                                 kparts[16 * p:16 * p + 16, K_PART[s], :]).then_inc(k_in[p], 16)

            def load_ctx(b, c):
                sp.wait_ge(ctxT_ps, CHUNKS * (b - 1) + c + 1)
                sp.dma_start(ctx_sb[:, 4 * c:4 * c + 4, :],
                             ctx[b % B, 512 * c:512 * c + 512, :].rearrange("(t k) d -> k t d", k=128)).then_inc(in_ctx[c], 16)

            sp.wait_ge(qpair_ready, 2)
            sp.dma_start(q_scratch[:, :, 0, :], qpair[:, :, 0, :, :].rearrange("p i h s -> p i (h s)")).then_inc(q_out0, 16)
            sp.wait_ge(q_out0, 16)
            load_q(0)
            sp.wait_ge(k1_ready, CHUNKS)
            load_k(0, 0, range(0, 3))
            sp.wait_ge(k2_ready, CHUNKS)
            load_k(0, 0, range(3, 5))
            sp.wait_ge(k3_ready, CHUNKS)
            load_k(0, 0, range(5, 6))
            load_k(0, 1)
            for c in range(CHUNKS):
                load_ctx(1, c)
            load_k(0, 2)
            sp.dma_start(rows[:].rearrange("p r d -> p (r d)"), bias_rows.partition_broadcast(128)).then_inc(in_rows, 16)
            sp.wait_ge(qpair_ready, 4)
            sp.dma_start(q_scratch[:, :, 1:B, :], qpair[:, :, 1:B, :, :].rearrange("p i b h s -> p i b (h s)")).then_inc(q_out, 16)
            sp.dma_start(q_full, qf[:]).then_inc(q_saved, 16)
            for p in range(3, PAIRS):
                load_k(0, p)
            sp.wait_ge(q_out, 16)
            for b in range(1, B):
                load_q(b)
            for dst, src in ((wo_sb, w_o), (aq_sb, a_wqT), (ak_sb, a_wkT), (av_sb, a_wvT)):
                sp.dma_start(dst[:], src).then_inc(in_tail, 16)
            for b in range(1, B):
                if b + 1 < B:
                    for c in range(CHUNKS):
                        load_ctx(b + 1, c)
                sp.wait_ge(k3_ready, CHUNKS * (b + 1))
                for p in range(PAIRS):
                    if b >= 2:
                        sp.wait_ge(b_ps, STEPS * ((b - 2) * PAIRS + p + 1))
                    load_k(b, p)

            def store(turn):
                for b in range(B):
                    sp.wait_ge(y_ready, B * turn + b + 1)
                    sp.dma_start(out[b], y_sb[:, b, :]).then_inc(y_out, 16)
                sp.wait_ge(y_out, 16 * B * (turn + 1))

            store(0)
            with masked(sp):
                sp.dma_start(g_q, q_full).then_inc(g_in_q, 16)
                for b in range(B):
                    for c in range(CHUNKS):
                        load_ctx(B + b, c)
                    if b >= 1:
                        sp.wait_ge(g_mask_read, b)
                    sp.dma_start(g_mask.bitcast(I32), mask[b, 0]).then_inc(g_in_mask, 16)
                store(1)

        @block.gpsimd
        def _(gp):
            link = chain_of(gp, pool)
            link(nc.gpsimd.memset(ident[:], 0.0))
            link(nc.gpsimd.affine_select(out=ident[:], in_=ident[:], compare_op=ALU.not_equal, fill=1.0, base=0,
                                         pattern=[[-1, 128]], channel_multiplier=1))
            nc.gpsimd.tensor_copy(identb[:], ident[:]).then_inc(consts, 1)
            nc.gpsimd.memset(neg_half[:], -0.5).then_inc(consts, 1)
            nc.gpsimd.memset(ones_rows[:], 1.0019378662109375).then_inc(consts, 1)
            gp.wait_ge(consts, 3)
            for i, (b0, b1) in enumerate(PHASES):
                gp.wait_ge(var_ready, i + 1)
                nc.gpsimd.tensor_tensor(rstd[:, b0:b1], moments[:, b0:b1, 1], neg_half[:, b0:b1],
                                        ALU.pow).then_inc(rstd_ready, 1)
            link(nc.gpsimd.memset(vt[:, :, :, :, DK:DK + 1], 1.0))
            gp.dma_start(up_y[:, 0, :], w_exp).then_inc(in_ffn, 16)
            gp.dma_start(down_y[:, STAGES % 2, :], w_conT).then_inc(in_ffn, 16)
            gp.dma_start(row_y[:, 0, :], b_exp).then_inc(in_ffn, 16)
            gp.dma_start(ub_row[:], up_bias).then_inc(in_ffn, 16)

            def split_third(b, c):
                n = CHUNKS * b + c
                gp.wait_ge(k2_ready, n + 1)
                sl = slice(512 * c, 512 * c + 512)
                nc.gpsimd.tensor_tensor(kparts[:, 2, sl], krest[:, c % 2, :], kparts[:, 1, sl],
                                        ALU.subtract).then_inc(k3_ready, 1)

            def split_max(g):
                i = g % 2
                gp.wait_ge(negmax_ready, g + 1)
                if g >= 2:
                    gp.wait_ge(m_ps, g - 1)
                link(nc.gpsimd.tensor_copy(mparts[:, i, :, 0], negmax[:, i, :]))
                link(nc.gpsimd.tensor_tensor(mrest[:, i, :], negmax[:, i, :], mparts[:, i, :, 0], ALU.subtract))
                link(nc.gpsimd.tensor_copy(mparts[:, i, :, 1], mrest[:, i, :]))
                nc.gpsimd.tensor_tensor(mparts[:, i, :, 2], mrest[:, i, :], mparts[:, i, :, 1],
                                        ALU.subtract).then_inc(mparts_ready, 1)

            def load_stage(n):
                src = w_up[n] if n < STAGES else w_down[2 * STAGES - 1 - n]
                gp.dma_start(stage_w[:, n % 2, :], src.partition_broadcast(128)).then_inc(in_stage[n % 2], 16)

            def butterfly(n, y, parts):
                s = 2 ** (n if n < STAGES else 2 * STAGES - 1 - n)
                w = stage_w[0:parts, n % 2, :].rearrange("p (n s i j) -> p n i j s", s=s, i=2, j=2)
                yr = y[0:parts, n % 2, :].rearrange("p (n i s) -> p n i s", i=2, s=s)
                shape = [parts, HID // (2 * s), 2, s]
                first, second = (yr[:, :, e:e + 1, :].broadcast_to(shape) for e in range(2))
                w0, w1 = (w[:, :, :, e, :] if n < STAGES else w[:, :, e, :, :] for e in range(2))
                va, vb = (t[0:parts, :].rearrange("p (n i s) -> p n i s", i=2, s=s) for t in (bf_a, bf_b))
                link(nc.gpsimd.tensor_tensor(va, w0, first, ALU.mult), wait=False)
                link(nc.gpsimd.tensor_tensor(vb, w1, second, ALU.mult))
                link(nc.gpsimd.tensor_tensor(y[0:parts, (n + 1) % 2, :], bf_a[0:parts, :], bf_b[0:parts, :], ALU.add))

            def stage_part(i):
                n, row = divmod(i, 2) if i < 2 * STAGES else (i - STAGES, 0)
                if row:
                    butterfly(n, row_y, 1)
                else:
                    gp.wait_ge(in_stage[n % 2], 16 * (n // 2 + 1))
                    if n == 0:
                        gp.wait_ge(in_ffn, 64)
                        gp.wait_ge(qpair_ready, 4)
                        gp.wait_ge(q_saved, 16)
                    butterfly(n, up_y if n < STAGES else down_y, 128)
                if n == STAGES - 1 and row:
                    nc.gpsimd.tensor_tensor(up_b, row_y[:, STAGES % 2, :], ub_row[:], ALU.add).then_inc(up_b_ready, 1)
                if n + 2 < 2 * STAGES and (row or n >= STAGES):
                    load_stage(n + 2)
                if i == 3 * STAGES - 1:
                    gp.wait_ge(in_rows, 16)
                    nc.gpsimd.tensor_tensor(out_bias[:], rows[:, 2, :], rows[:, 3, :], ALU.add).then_inc(down_ready, 1)

            def power(i):
                gp.wait_ge(t_var, i + 1)
                nc.gpsimd.tensor_tensor(t_rstd[:], t_mom[:, 1:2], neg_half[:, 0:1], ALU.pow).then_inc(t_rs, 1)

            load_stage(0)
            load_stage(1)
            for c in range(CHUNKS):
                split_third(0, c)
            split_max(0)
            for g in range(G):
                b, p = divmod(g, PAIRS)
                if g + 1 < G:
                    split_max(g + 1)
                if b > 0 and p in (2, 5):
                    power(2 * (b - 1) + (p == 5))
                if g < 3 * STAGES:
                    stage_part(g)
                if b + 1 < B and p < CHUNKS:
                    split_third(b + 1, p)
            power(2 * (B - 1))
            power(2 * (B - 1) + 1)
            with masked(gp):
                for b in range(B, 2 * B):
                    power(2 * b)
                    power(2 * b + 1)

        @block.scalar
        def _(act_e):
            link = chain_of(act_e, act)

            def take(task, src):
                kind, b, what, c = task
                n = CHUNKS * b + c
                sl = slice(512 * c, 512 * c + 512)
                if what == "turn":
                    act_e.wait_ge(ctxT_ps, n + 1)
                    nc.scalar.copy(ctxT[:, sl], src).then_inc(ctxT_ready, 1)
                elif what == "k" and b >= B:
                    act_e.wait_ge(k_ps, n + 1)
                    nc.scalar.activation(g_kT[:, sl], src, ACT.Identity, bias=cols[:, 1:2]).then_inc(g_k_ready, 1)
                elif what == "v" and b >= B:
                    act_e.wait_ge(v_ps, n + 1)
                    nc.scalar.copy(g_v[:, sl], src).then_inc(v_ready, 1)
                elif kind == "flag":
                    return
                elif what == "k":
                    act_e.wait_ge(k_ps, n + 1)
                    if b == 0:
                        act_e.wait_ge(in_wk, 32)
                    elif c == 0:
                        for p in range(PAIRS):
                            act_e.wait_ge(k_in[p], 16 * SLOTS * b)
                    nc.scalar.activation(kparts[:, 0, sl], src, ACT.Identity, bias=cols[:, 1:2]).then_inc(k1_ready, 1)
                elif what == "v":
                    act_e.wait_ge(v_ps, n + 1)
                    if b >= 2:
                        act_e.wait_ge(pv_done, STEPS * PAIRS * (b - 1))
                    nc.scalar.copy(vt[:, b % 2, 4 * c:4 * c + 4, :, 0:DK],
                                   src.rearrange("p (t h d) -> p t h d", t=4, h=H)).then_inc(v_ready, 1)
                else:
                    if what in ("project", "self_out"):
                        return
                    act_e.wait_ge(tail_ps, len(TAIL) * b + TAIL.index(what) + 1)
                    if what == "turn_att":
                        nc.scalar.activation(attT[:], src[:, 0:S], ACT.Identity, bias=cols[:, 2:3]).then_inc(tail_sb, 1)
                    elif what == "turn_x1":
                        nc.scalar.copy(t_xnT[:], src[:, 0:S]).then_inc(tail_sb, 1)
                    elif what == "qkv":
                        link(nc.scalar.activation(s_qT[:], src[:, 0:S], ACT.Identity, bias=abq_s[:], scale=float(D) ** -0.5), wait=False)
                        link(nc.scalar.activation(s_kT[:], src[:, S:2 * S], ACT.Identity, bias=cols[:, 4:5]), wait=False)
                        nc.scalar.copy(s_v[:], src[:, 2 * S:2 * S + D]).then_inc(tail_sb, 1)
                    elif what == "scores":
                        act_e.wait_ge(s_max_ready, b + 1)
                        nc.scalar.activation(s_p[:], src[:, 0:S], ACT.Exp, bias=s_negmax[:],
                                             accum_out=s_sum[:]).then_inc(tail_sb, 1)
                    elif what == "turn_p":
                        nc.scalar.copy(s_pT[:], src[:, 0:S]).then_inc(tail_sb, 1)
                    elif what == "turn_x2":
                        nc.scalar.copy(f_xnT[:, S * (b % B):S * (b % B) + S], src[:, 0:S]).then_inc(tail_sb, 1)

            def exp_step(u):
                act_e.wait_ge(b_ps, u + 1)
                if u >= 4:
                    act_e.wait_ge(pv_done, u - 3)
                nc.scalar.activation(probs[:, u % 4, :], ps_b[:, u % 3, :], ACT.Exp).then_inc(p_ready, 1)

            def take_outputs(g):
                act_e.wait_ge(pv_done, STEPS * (g + 1))
                if g >= 2:
                    act_e.wait_ge(o_ps, g - 1)
                nc.scalar.copy(oT[:, g % 2, :], ps_o[:, g % 2, 0:S]).then_inc(oT_ready, 1)

            def place_max(g):
                act_e.wait_ge(m_ps, g + 1)
                nc.scalar.copy(qstack[ROWS:ROWS + MROWS, g // PAIRS, g % PAIRS, :],
                               ps_o[ROWS:ROWS + MROWS, g % 2, 256:384].bitcast(BF16)).then_inc(m_ready, 1)

            def load_mask(i):
                if i == 0:
                    act_e.wait_ge(q_out, 16)
                if i >= MRING:
                    act_e.wait_ge(mask_read, i - MRING + 1)
                act_e.dma_start(mask_sb[:, i % MRING, :], mask[i // CHUNKS, 0, :, 512 * (i % CHUNKS):512 * (i % CHUNKS) + 512]
                                ).then_inc(mask_in[i % MRING], 16)

            def take_xn(i):
                b0, b1 = PHASES[i]
                act_e.wait_ge(xnT_ps, i + 1)
                nc.scalar.copy(xnT[:, S * b0:S * b1], ps_m[:, S * b0:S * b1]).then_inc(xnT_ready, 1)

            take(("prep", 0, "turn", 0), ps_b[:, 0, :])
            take_xn(0)
            for c in range(CHUNKS):
                take(("prep", 0, "k", c), K_BANK[c])
                if c == 0:
                    take_xn(1)
                if c + 1 < CHUNKS:
                    take(("prep", 0, "turn", c + 1), ps_b[:, (c + 1) % 3, :])
            link(nc.scalar.mul(abq_s[:], cols[:, 3:4], float(D) ** -0.5))
            for c in range(CHUNKS):
                take(("prep", 0, "v", c), V_BANK[c])
            place_max(0)
            for g in range(G):
                for k in range(STEPS):
                    exp_step(STEPS * g + k)
                    if k == 0 and 0 <= g - 4 < B * CHUNKS:
                        load_mask(g - 4)
                    if k == 2 and g >= 1:
                        take_outputs(g - 1)
                    if k == 5 and g + 1 < G:
                        place_max(g + 1)
                    if k % 2 == 1 and misc_task(g, k - 1):
                        take(misc_task(g, k - 1), ps_m[:])
            take_outputs(G - 1)

            def tail(b):
                for what in TAIL:
                    take(("tail", b, what, 0), ps_m[:])

            def hidden(turn):
                act_e.wait_ge(up_bcol_ready, 1)
                for j in range(HB):
                    act_e.wait_ge(up_ps, HB * turn + j + 1)
                    src = ps_b[:, j, :] if j < 3 else ps_a[:, 0, :]
                    nc.scalar.activation(f_h[:, j, :], src, ACT.Gelu, bias=up_bcol[:, j:j + 1]).then_inc(gelu_ready, 1)

            tail(B - 1)
            hidden(0)
            with masked(act_e):
                act_e.wait_ge(y_out, 16 * B)
                for b in range(B):
                    for what, c in PREP:
                        take(("prep", B + b, what, c), ps_m[:])
                    with act_e.Fori(0, H) as h:
                        n = h + H * b + 1
                        act_e.wait_ge(g_max_ready, n)
                        nc.scalar.activation(g_s, g_s, ACT.Exp, bias=g_negmax, accum_out=g_sum).then_inc(g_p_ready, 1)
                        act_e.wait_ge(g_pT_ps, n)
                        for c in range(CHUNKS):
                            ins = nc.scalar.copy(g_pT[:, 512 * c:512 * c + 512], g_bank(c))
                        ins.then_inc(g_pT_ready, 1)
                    tail(B + b)
                hidden(1)

        @block.vector
        def _(ve):
            link = chain_of(ve, dve)

            def norm_stats(src, st, mom, done):
                link(nc.vector.bn_stats(st, src))
                link(nc.vector.bn_aggr(mom, st))
                nc.vector.tensor_scalar_add(mom[:, 1:2], mom[:, 1:2], EPS).then_inc(done, 1)

            def split_k(b, c, src):
                n = CHUNKS * b + c
                sl = slice(512 * c, 512 * c + 512)
                ve.wait_ge(k1_ready, n + 1)
                if n >= 2:
                    ve.wait_ge(k3_ready, n - 1)
                link(nc.vector.scalar_tensor_tensor(out=krest[:, c % 2, :], in0=src, scalar=cols[:, 1:2],
                                                    in1=kparts[:, 0, sl], op0=ALU.add, op1=ALU.subtract))
                nc.vector.tensor_copy(kparts[:, 1, sl], krest[:, c % 2, :]).then_inc(k2_ready, 1)

            def chunk_max(ua):
                g, k = divmod(ua, STEPS)
                ve.wait_ge(a_ps, ua + 1)
                nc.vector.tensor_reduce(smax[:, g % 2, k // CHUNKS, k % CHUNKS:k % CHUNKS + 1], ps_a[:, ua % 2, :],
                                        AX.X, ALU.max).then_inc(a_max, 1)

            def row_max(g):
                ve.wait_ge(a_max, STEPS * (g + 1))
                if g >= 2:
                    ve.wait_ge(mparts_ready, g - 1)
                nc.vector.tensor_reduce(negmax[:, g % 2, :], smax[:, g % 2, :, :], AX.X, ALU.max,
                                        negate=True).then_inc(negmax_ready, 1)

            def sum_outputs(g):
                ve.wait_ge(o_ps, g + 1)
                src = ps_o[:, g % 2, 128:256].rearrange("q (e h r) -> q h r e", e=2, h=2)[:, :, 0:DK + 1, :]
                nc.vector.tensor_reduce(osum[:, (g // PAIRS) % 2, g % PAIRS, :, :], src, AX.X, ALU.add).then_inc(osum_ready, 1)

            def normalise(b):
                if b < B:
                    ve.wait_ge(osum_ready, PAIRS * (b + 1))
                if b >= 1:
                    ve.wait_ge(tail_ps, len(TAIL) * (b - 1) + 1)
                i = b % 2
                link(nc.vector.reciprocal(rsum[:, i, :, :], osum[:, i, :, :, DK]))
                nc.vector.tensor_tensor(att[:].rearrange("q (p h d) -> q p h d", p=PAIRS, h=2), osum[:, i, :, :, 0:DK],
                                        rsum[:, i, :, :].unsqueeze(3).broadcast_to([128, PAIRS, 2, DK]),
                                        ALU.mult).then_inc(att_ready, 1)

            def take(task, src):
                kind, b, what, c = task
                if what == "k" and b < B:
                    split_k(b, c, src)
                    return
                if kind == "flag":
                    ve.wait_ge(low_ps, 1)
                    nc.vector.tensor_reduce(flag_f[:], src[0:1, 0:128], AX.X, ALU.min).then_inc(low_read, 1)
                    ve.wait_ge(low_read, 1)
                    nc.vector.tensor_scalar(flag[:], flag_f[:], 0.0, None, ALU.is_equal).then_inc(flag_ready, 1)
                    return
                if kind == "prep" or what not in ("project", "scores", "self_out"):
                    return
                ve.wait_ge(tail_ps, len(TAIL) * b + TAIL.index(what) + 1)
                if what == "project":
                    nc.vector.tensor_tensor(x1[:], src[:, 0:D], xo_sb[:, b % B, :], ALU.add).then_inc(tail_sb, 1)
                    ve.wait_ge(tail_sb, len(TAIL) * b + TAIL.index(what) + 1)
                    link(nc.vector.tensor_tensor(x1v[:], x1[:], rows[:, 1, :], ALU.add), wait=False)
                    norm_stats(x1[:], t_stats[:], t_mom[:], t_var)
                elif what == "scores":
                    nc.vector.tensor_reduce(s_negmax[:], src[:, 0:S], AX.X, ALU.max, negate=True).then_inc(s_max_ready, 1)
                elif what == "self_out":
                    link(nc.vector.reciprocal(s_rsum[:], s_sum[:]))
                    nc.vector.scalar_tensor_tensor(out=x2[:, b % B, :], in0=src[:, 0:D], scalar=s_rsum[:], in1=x1v[:],
                                                   op0=ALU.mult, op1=ALU.add).then_inc(tail_sb, 1)
                    ve.wait_ge(tail_sb, len(TAIL) * b + TAIL.index(what) + 1)
                    norm_stats(x2[:, b % B, :], t_stats[:], t_mom[:], t_var)

            def tail_norm(b, second):
                ve.wait_ge(t_rs, 2 * b + second + 1)
                nc.vector.tensor_scalar(t_xn[:], x2[:, b % B, :] if second else x1[:], t_mom[:, 0:1], t_rstd[:],
                                        ALU.subtract, ALU.mult).then_inc(t_xn_ready, 1)

            def search_mask(i):
                ve.wait_ge(mask_in[i % MRING], 16 * (i // MRING + 1))
                nc.vector.tensor_reduce(mask_min[:, i:i + 1], mask_sb[:, i % MRING, :], AX.X, ALU.min,
                                        apply_absolute_value=True).then_inc(mask_read, 1)

            def split_q(i):
                b0, b1 = PHASES[i]
                sl = slice(S * b0, S * b1)
                ve.wait_ge(q_ps, i + 1)
                link(nc.vector.tensor_scalar(qf[:, sl], ps_o[:, 0, sl], cols[:, 0:1], float(DK) ** -0.5, ALU.add, ALU.mult))
                link(nc.vector.tensor_copy(qparts[:, 0, sl], qf[:, sl]))
                link(nc.vector.tensor_tensor(qrest[:, sl], qf[:, sl], qparts[:, 0, sl], ALU.subtract))
                link(nc.vector.tensor_copy(qparts[:, 1, sl], qrest[:, sl]))
                link(nc.vector.tensor_tensor(qparts[:, 2, sl], qrest[:, sl], qparts[:, 1, sl], ALU.subtract))
                for j in range(2):
                    nc.vector.tensor_scalar(qpair[:, :, b0:b1, j, :], qparts[:, :, sl].rearrange("p i (b s) -> p i b s", s=S),
                                            parity[:, j:j + 1], None, ALU.mult).then_inc(qpair_ready, 1)

            for i, (b0, b1) in enumerate(PHASES):
                ve.wait_ge((in_x, in_x1)[i], 16)
                for b in range(b0, b1):
                    link(nc.vector.bn_stats(stats[:, b, :], x_sb[:, b, :]), wait=(b == b1 - 1))
                for b in range(b0, b1):
                    link(nc.vector.bn_aggr(moments[:, b, :], stats[:, b, :]), wait=(b == b1 - 1))
                nc.vector.tensor_scalar_add(moments[:, b0:b1, 1], moments[:, b0:b1, 1], EPS).then_inc(var_ready, 1)
                if i == 0:
                    ve.wait_ge(consts, 1)
                    link(nc.vector.tensor_reduce(parity[:], ident[:].rearrange("p (a j d) -> p j a d", j=2, d=DK),
                                                 AX.XY, ALU.add), wait=False)
                ve.wait_ge(rstd_ready, i + 1)
                for b in range(b0, b1):
                    nc.vector.tensor_scalar(xn[:, b, :], x_sb[:, b, :], moments[:, b, 0:1], rstd[:, b:b + 1],
                                            ALU.subtract, ALU.mult).then_inc(xn_ready, 1)
                if i == 0:
                    ve.wait_ge(in_wk, 32)
                    split_q(0)
            for c in range(CHUNKS):
                split_k(0, c, K_BANK[c])
            split_q(1)
            for i in range(2):
                nc.vector.memset(ps_o[:, i, 0:S], 0.0).then_inc(o_clear, 1)
            for ua in range(AHEAD * STEPS):
                chunk_max(ua)
                if ua == STEPS - 1:
                    row_max(0)
            for g in range(G):
                b, p = divmod(g, PAIRS)
                for k in range(STEPS):
                    if g + AHEAD < G:
                        chunk_max(STEPS * (g + AHEAD) + k)
                    if k == 0 and g + 1 < G:
                        row_max(g + 1)
                    if k == 7 and g >= 1:
                        sum_outputs(g - 1)
                    if (g, k) == (1, 2):
                        ve.wait_ge(in_rows, 16)
                        link(nc.vector.tensor_tensor(xo_sb[:], x_sb[:], rows[:, 0:1, :].broadcast_to([128, B, D]), ALU.add),
                             wait=False)
                    if k == 0 and b > 0 and p == 1:
                        normalise(b - 1)
                    if k == 3 and 0 <= g - 5 < B * CHUNKS:
                        search_mask(g - 5)
                    if (b, p, k) == (B - 1, 0, 0):
                        ve.wait_ge(mask_read, B * CHUNKS)
                        nc.vector.tensor_reduce(mask_low[:], mask_min[:], AX.X, ALU.min).then_inc(low_ready, 1)
                    if b > 0 and (p, k) in ((2, 5), (5, 5)):
                        tail_norm(b - 1, p == 5)
                    if k % 2 == 1 and misc_task(g, k - 1):
                        take(misc_task(g, k - 1), ps_m[:])
            sum_outputs(G - 1)
            normalise(B - 1)

            def tail(b):
                for what in TAIL:
                    if what in ("turn_x1", "turn_x2"):
                        tail_norm(b, what == "turn_x2")
                    take(("tail", b, what, 0), ps_m[:])

            def result(turn):
                link(nc.vector.tensor_tensor(x2b[:], x2[:], out_bias[:].unsqueeze(1).broadcast_to([128, B, D]), ALU.add))
                for b in range(B):
                    ve.wait_ge(dn_ps, B * turn + b + 1)
                    src = (ps_a[:, 1, 0:D], ps_m[:, 0:D])[b % 2]
                    nc.vector.tensor_tensor(y_sb[:, b, :], src, x2b[:, b, :], ALU.add).then_inc(y_ready, 1)

            tail(B - 1)
            ve.wait_ge(down_ready, 1)
            ve.wait_ge(up_bps, 1)
            nc.vector.tensor_copy(up_bcol[:], ps_o[:, 0, 0:HB]).then_inc(up_bcol_ready, 1)
            ve.wait_ge(dn_tps, 1)
            nc.vector.tensor_copy(xnT[:], ps_o[:, 1, :]).then_inc(w_dn_ready, 1)
            result(0)
            with masked(ve):
                ve.wait_ge(y_out, 16 * B)
                link(nc.vector.tensor_reduce(g_heads, ident[:].rearrange("p (h d) -> p h d", d=DK), AX.X, ALU.add))
                ve.wait_ge(g_in_q, 16)
                for b in range(B):
                    ve.wait_ge(g_in_mask, 16 * (b + 1))
                    nc.vector.tensor_scalar(g_drop, g_mask.bitcast(I32), 0.0, None, ALU.is_equal).then_inc(g_mask_read, 1)
                    ve.wait_ge(g_mask_read, b + 1)
                    link(nc.vector.tensor_scalar(g_keep, g_drop, -1.0, 1.0, ALU.mult, ALU.add))
                    LINKS = 2 * CHUNKS
                    with ve.Fori(0, H) as h:
                        n = h + H * b + 1
                        nc.vector.tensor_scalar(g_qh, g_q[:, S * b:S * b + S], g_heads[:, bass.ds(h, 1)], None,
                                                ALU.mult).then_inc(g_qh_ready, 1)
                        ve.wait_ge(g_s_ps, n)
                        for c in range(CHUNKS):
                            sl = slice(512 * c, 512 * c + 512)
                            nc.vector.tensor_tensor(g_s[:, sl], g_bank(c), g_keep[:, sl], ALU.mult).then_inc(g_dve, 1)
                            ve.wait_ge(g_dve, (n - 1) * LINKS + 2 * c + 1)
                            nc.vector.scalar_tensor_tensor(out=g_s[:, sl], in0=g_drop[:, sl], scalar=-1e9, in1=g_s[:, sl],
                                                           op0=ALU.mult, op1=ALU.add).then_inc(g_dve, 1)
                        ve.wait_ge(g_dve, n * LINKS)
                        nc.vector.tensor_reduce(g_negmax, g_s, AX.X, ALU.max, negate=True).then_inc(g_max_ready, 1)
                        ve.wait_ge(g_o_ps, n)
                        sums = osum[:, b % 2, :, :, :].rearrange("q p h r -> q (p h) r")
                        nc.vector.tensor_copy(sums[:, bass.ds(h, 1), 0:DK], ps_m[:, 0:DK].unsqueeze(1)).then_inc(g_o_read, 1)
                        nc.vector.tensor_copy(sums[:, bass.ds(h, 1), DK:DK + 1], g_sum.unsqueeze(1)).then_inc(g_o_read, 1)
                    ve.wait_ge(g_o_read, 2 * H * (b + 1))
                    normalise(B + b)
                    tail(B + b)
                result(1)

        @block.tensor
        def _(pe):
            def put(task, dst):
                kind, b, what, c = task
                n = CHUNKS * b + c
                if kind == "flag":
                    pe.wait_ge(low_ready, 1)
                    nc.tensor.transpose(dst[0:1, 0:128], mask_low[:], ident[:]).then_inc(low_ps, 1)
                elif what == "turn":
                    pe.wait_ge(in_ctx[c], 16 * (b + 1))
                    for t in range(4):
                        ins = nc.tensor.transpose(dst[:, 128 * t:128 * t + 128], ctx_sb[:, 4 * c + t, :], ident[:])
                    ins.then_inc(ctxT_ps, 1)
                elif what == "k":
                    pe.wait_ge(ctxT_ready, n + 1)
                    pe.wait_ge(in_wk, 32)
                    nc.tensor.matmul(dst, wk_sb[:], ctxT[:, 512 * c:512 * c + 512], start=True, stop=True).then_inc(k_ps, 1)
                elif what == "v":
                    pe.wait_ge(ctxT_ready, n + 1)
                    pe.wait_ge(in_wv, 16)
                    for t in range(4):
                        key = 512 * c + 128 * t
                        ins = nc.tensor.matmul(dst[:, 128 * t:128 * t + 128], ctxT[:, key:key + 128], wv_sb[:],
                                               start=True, stop=True)
                    ins.then_inc(v_ps, 1)
                elif what == "turn_att":
                    pe.wait_ge(att_ready, b + 1)
                    nc.tensor.transpose(dst[:, 0:S], att[:], ident[:]).then_inc(tail_ps, 1)
                elif what == "project":
                    pe.wait_ge(in_tail, 64)
                    nc.tensor.matmul(dst[:, 0:D], attT[:], wo_sb[:], start=True, stop=True).then_inc(tail_ps, 1)
                elif what in ("turn_x1", "turn_x2"):
                    pe.wait_ge(t_xn_ready, 2 * b + 1 + (what == "turn_x2"))
                    nc.tensor.transpose(dst[:, 0:S], t_xn[:], ident[:]).then_inc(tail_ps, 1)
                elif what == "qkv":
                    nc.tensor.matmul(dst[:, 0:S], aq_sb[:], t_xnT[:], start=True, stop=True)
                    nc.tensor.matmul(dst[:, S:2 * S], ak_sb[:], t_xnT[:], start=True, stop=True)
                    nc.tensor.matmul(dst[:, 2 * S:2 * S + D], t_xnT[:], av_sb[:], start=True, stop=True).then_inc(tail_ps, 1)
                elif what == "scores":
                    nc.tensor.matmul(dst[:, 0:S], s_qT[:], s_kT[:], start=True, stop=True).then_inc(tail_ps, 1)
                elif what == "turn_p":
                    nc.tensor.transpose(dst[:, 0:S], s_p[:], ident[:]).then_inc(tail_ps, 1)
                elif what == "self_out":
                    nc.tensor.matmul(dst[:, 0:D], s_pT[:], s_v[:], start=True, stop=True).then_inc(tail_ps, 1)

            def put_misc(task):
                pe.wait_ge(*before[task])
                if task[0] == "tail" and task[2] != TAIL[0]:
                    pe.wait_ge(tail_sb, len(TAIL) * task[1] + TAIL.index(task[2]))
                put(task, ps_m[:])

            def scores_by_query(ua):
                g, k = divmod(ua, STEPS)
                b, p = divmod(g, PAIRS)
                if k == 0:
                    pe.wait_ge(k_in[p], 16 * SLOTS * (b + 1))
                    pe.wait_ge(q_in[b], 16 * SLOTS)
                if ua >= 2:
                    pe.wait_ge(a_max, ua - 1)
                h, c = divmod(k, CHUNKS)
                nc.tensor.matmul(ps_a[:, ua % 2, :], qstack[0:ROWS, b, p, S * h:S * h + S],
                                 kstack[0:ROWS, b % 2, p, 512 * c:512 * c + 512], start=True, stop=True).then_inc(a_ps, 1)

            def scores_by_key(u):
                g, k = divmod(u, STEPS)
                b, p = divmod(g, PAIRS)
                if k == 0:
                    pe.wait_ge(m_ready, g + 1)
                    if g == 0:
                        pe.wait_ge(ones_in, 16 * 2)
                if u >= 3:
                    pe.wait_ge(p_ready, u - 2)
                for e in range(2):
                    key = 128 * (2 * k + e)
                    ins = nc.tensor.matmul(ps_b[:, u % 3, 256 * e:256 * e + 256],
                                           kstack[0:ROWS + MROWS, b % 2, p, key:key + 128],
                                           qstack[0:ROWS + MROWS, b, p, :], start=True, stop=True)
                ins.then_inc(b_ps, 1)

            def outputs(u):
                g, k = divmod(u, STEPS)
                b, p = divmod(g, PAIRS)
                pe.wait_ge(p_ready, u + 1)
                if k == 0:
                    if p == 0:
                        pe.wait_ge(v_ready, CHUNKS * (b + 1))
                    if g == 0:
                        pe.wait_ge(o_clear, 2)
                    if g >= 2:
                        pe.wait_ge(osum_ready, g - 1)
                for e in range(2):
                    for h in range(2):
                        j = 2 * e + h
                        ins = nc.tensor.matmul(ps_o[32 * j:32 * j + DK + 1, g % 2, 0:S],
                                               vt[:, b % 2, 2 * k + e, 2 * p + h, :],
                                               probs[:, u % 4, 128 * j:128 * j + 128],
                                               start=(k == 0), stop=(k == STEPS - 1))
                ins.then_inc(pv_done, 1)

            def turn_outputs(g):
                pe.wait_ge(oT_ready, g + 1)
                if g + 2 < G:
                    pe.wait_ge(m_ready, g + 3)
                nc.tensor.transpose(ps_o[:, g % 2, 128:256], oT[:, g % 2, :], ident[:]).then_inc(o_ps, 1)

            def turn_max(g):
                pe.wait_ge(mparts_ready, g + 1)
                if g >= 2:
                    pe.wait_ge(oT_ready, g - 1)
                for h in range(2):
                    ins = nc.tensor.transpose(ps_o[ROWS:ROWS + MROWS, g % 2, 256 + 64 * h:320 + 64 * h].bitcast(BF16),
                                              mparts[:, g % 2, h, :], identb[:])
                ins.then_inc(m_ps, 1)

            def turn_xn(i):
                for b in range(*PHASES[i]):
                    pe.wait_ge(xn_ready, b + 1)
                    ins = nc.tensor.transpose(ps_m[:, S * b:S * b + S], xn[:, b, :], ident[:])
                ins.then_inc(xnT_ps, 1)

            def project_q(i):
                sl = slice(S * PHASES[i][0], S * PHASES[i][1])
                pe.wait_ge(xnT_ready, i + 1)
                nc.tensor.matmul(ps_o[:, 0, sl], wq_sb[:], xnT[:, sl], start=True, stop=True).then_inc(q_ps, 1)

            pe.wait_ge(consts, 1)
            put(("prep", 0, "turn", 0), ps_b[:, 0, :])
            turn_xn(0)
            pe.wait_ge(in_wq, 16)
            project_q(0)
            put(("prep", 0, "k", 0), K_BANK[0])
            turn_xn(1)
            for c in range(1, CHUNKS):
                if c == 3:
                    pe.wait_ge(ctxT_ready, 1)
                put(("prep", 0, "turn", c), ps_b[:, c % 3, :])
                if c == 1:
                    project_q(1)
                put(("prep", 0, "k", c), K_BANK[c])
            for c in range(CHUNKS):
                if c == 1:
                    pe.wait_ge(ctxT_ready, CHUNKS)
                if c == 3:
                    pe.wait_ge(v_ready, 1)
                put(("prep", 0, "v", c), V_BANK[c])
            pe.wait_ge(k2_ready, CHUNKS)
            for ua in range(AHEAD * STEPS):
                scores_by_query(ua)
            pe.wait_ge(o_clear, 2)
            pe.wait_ge(v_ready, CHUNKS)
            turn_max(0)
            for g in range(G):
                for k in range(STEPS):
                    u = STEPS * g + k
                    scores_by_key(u)
                    if g + AHEAD < G:
                        scores_by_query(STEPS * (g + AHEAD) + k)
                    if u >= LAG:
                        outputs(u - LAG)
                    if k == 4 and g + 1 < G:
                        turn_max(g + 1)
                    if k == 6 and g >= 1:
                        turn_outputs(g - 1)
                    if misc_task(g, k):
                        put_misc(misc_task(g, k))
            for u in range(STEPS * G - LAG, STEPS * G):
                outputs(u)
            turn_outputs(G - 1)
            pe.wait_ge(up_b_ready, 1)
            pe.wait_ge(osum_ready, G)
            for j in range(HB):
                ins = nc.tensor.matmul(ps_o[:, 0, j:j + 1], up_b[:, 128 * j:128 * j + 128], ident[0:1, 0:1],
                                       start=True, stop=True)
            ins.then_inc(up_bps, 1)
            pe.wait_ge(down_ready, 1)
            for j in range(HB):
                ins = nc.tensor.transpose(ps_o[:, 1, 128 * j:128 * j + 128], down_y[:, 0, 128 * j:128 * j + 128], ident[:])
            ins.then_inc(dn_tps, 1)

            def tail(b):
                for what in TAIL:
                    put_misc(("tail", b, what, 0))

            def feed_forward(turn):
                pe.wait_ge(tail_sb, len(TAIL) * B * (turn + 1))
                if turn == 0:
                    pe.wait_ge(p_ready, STEPS * G)
                for j in range(HB):
                    dst = ps_b[:, j, :] if j < 3 else ps_a[:, 0, :]
                    nc.tensor.matmul(dst, up_y[:, STAGES % 2, 128 * j:128 * j + 128], f_xnT[:],
                                     start=True, stop=True).then_inc(up_ps, 1)
                pe.wait_ge(w_dn_ready, 1)
                for b in range(B):
                    dst = (ps_a[:, 1, 0:D], ps_m[:, 0:D])[b % 2]
                    if b >= 2:
                        pe.wait_ge(y_ready, B * turn + b - 1)
                    for j in range(HB):
                        if b == 0:
                            pe.wait_ge(gelu_ready, HB * turn + j + 1)
                        ins = nc.tensor.matmul(dst, f_h[:, j, S * b:S * b + S], w_dn[:, j, :],
                                               start=(j == 0), stop=(j == HB - 1))
                    ins.then_inc(dn_ps, 1)

            tail(B - 1)
            feed_forward(0)
            with masked(pe):
                for b in range(B):
                    for what, c in PREP:
                        put_misc(("prep", B + b, what, c))
                    pe.wait_ge(g_k_ready, CHUNKS * (b + 1))
                    pe.wait_ge(v_ready, CHUNKS * (B + b + 1))
                    with pe.Fori(0, H) as h:
                        n = h + H * b + 1
                        pe.wait_ge(g_qh_ready, n)
                        for c in range(CHUNKS):
                            ins = nc.tensor.matmul(g_bank(c), g_qh, g_kT[:, 512 * c:512 * c + 512], start=True, stop=True)
                        ins.then_inc(g_s_ps, 1)
                        pe.wait_ge(g_p_ready, n)
                        for t in range(KT):
                            ins = nc.tensor.transpose(g_bank(t // 4)[:, 128 * (t % 4):128 * (t % 4) + 128],
                                                      g_s[:, 128 * t:128 * t + 128], ident[:])
                        ins.then_inc(g_pT_ps, 1)
                        pe.wait_ge(g_pT_ready, n)
                        for t in range(KT):
                            ins = nc.tensor.matmul(ps_m[:, 0:DK], g_pT[:, 128 * t:128 * t + 128],
                                                   g_v[:, bass.ds(h * DK + D * t, DK)], start=(t == 0), stop=(t == KT - 1))
                        ins.then_inc(g_o_ps, 1)
                    pe.wait_ge(g_o_read, 2 * H * (b + 1))
                    tail(B + b)
                feed_forward(1)


def kernel(**inputs):
    import numpy as np
    import concourse.bacc as bacc
    from concourse.bass_utils import run_bass_kernel_spmd

    def arr(name):
        return np.asarray(inputs[name])

    def flat(a):
        return a.reshape(1, -1)

    arrays = {
        "x": arr("x"),
        "ctx": arr("ctx_1024"),
        "mask": arr("mask_Bx1xSxS2_if1"),
        "w_q": arr("L0_xattn_Wq"), "w_k": arr("L0_xattn_Wk"), "w_v": arr("L0_xattn_Wv"), "w_o": arr("L0_xattn_Wo"),
        "a_wqT": arr("L0_attn_wq").T, "a_wkT": arr("L0_attn_wk").T, "a_wvT": arr("L0_attn_wv").T,
        "w_exp": arr("L0_ffn_W_exp"), "b_exp": flat(arr("L0_ffn_b_exp")),
        "w_up": arr("L0_ffn_up_weights").reshape(len(arr("L0_ffn_up_weights")), -1),
        "up_bias": flat(arr("L0_ffn_up_bias")),
        "w_down": arr("L0_ffn_down_weights").reshape(len(arr("L0_ffn_down_weights")), -1),
        "w_conT": arr("L0_ffn_W_con").T,
        "bias_cols": np.stack([arr(n) for n in ("L0_xattn_bq", "L0_xattn_bk", "L0_xattn_bv", "L0_attn_bq", "L0_attn_bk")], axis=1),
        "bias_rows": np.concatenate([arr(n) for n in ("L0_xattn_bo", "L0_attn_bv", "L0_ffn_b_con", "L0_ffn_down_bias")]),
    }
    arrays = {n: np.ascontiguousarray(a) for n, a in arrays.items()}
    nc = bacc.Bacc("TRN2", target_bir_lowering=False, num_devices=1)
    aps = [nc.dram_tensor(f"in_{n}", a.shape, mybir.dt.from_np(a.dtype), kind="ExternalInput").ap() for n, a in arrays.items()]
    shape = arrays["x"].shape
    out = nc.dram_tensor("out_x", shape, F32, kind="ExternalOutput").ap()
    q_scratch = nc.dram_tensor("q_scratch", (128, 3, shape[0], 2 * shape[1]), BF16).ap()
    q_full = nc.dram_tensor("q_full", (128, shape[0] * shape[1]), F32).ap()
    perceiver_block(nc, *aps, out, q_scratch, q_full)
    got = run_bass_kernel_spmd(nc, [{f"in_{n}": a for n, a in arrays.items()}], core_ids=[0])
    return got.results[0]["out_x"]
```

```python
from contextlib import ExitStack

import concourse.bass as bass
from concourse import mybir

F32 = mybir.dt.float32
BF16 = mybir.dt.bfloat16
I32 = mybir.dt.int32
ALU = mybir.AluOpType
ACT = mybir.ActivationFunctionType
AX = mybir.AxisListType

EPS = 1e-5
Q_PART = (0, 1, 2, 0, 1, 0)
K_PART = (0, 0, 0, 1, 1, 2)
SLOTS = len(Q_PART)


def perceiver_block(nc, x, ctx, mask, w_q, w_k, w_v, w_o, a_wqT, a_wkT, a_wvT, w_exp, b_exp, w_up,
                    up_bias, w_down, w_conT, bias_cols, bias_rows, out, q_scratch, q_full, row_scratch):
    B, S, D = x.shape
    KEYS = ctx.shape[1]
    H, DK = 16, 8
    KT = KEYS // 128
    PAIRS = H // 2
    G = B * PAIRS
    STEPS = KT // 2
    CHUNKS = KEYS // 512
    HID = w_exp.shape[1]
    HB = HID // 128
    STAGES = w_up.shape[0]
    ROWS = 16 * SLOTS
    MROWS = 3
    assert S == 128 and D == 128 and STEPS == 8 and CHUNKS == 4 and HB == 4

    with ExitStack() as es:
        def sb(name, shape, dt=F32):
            return es.enter_context(nc.sbuf_tensor(name, shape, dt))

        def psum(name, shape):
            return es.enter_context(nc.psum_tensor(name, shape, F32))

        def sem(name):
            return es.enter_context(nc.semaphore(name))

        x_sb = sb("x_sb", [128, B, D])
        xo_sb = sb("xo_sb", [128, B, D])
        xn = sb("xn", [128, B, D])
        stats = sb("stats", [128, B, 6])
        moments = sb("moments", [128, B, 2])
        rstd = sb("rstd", [128, B])
        neg_half = sb("neg_half", [128, B])
        xnT = sb("xnT", [128, B * S])
        qf = sb("qf", [128, B * S])
        qrest = sb("qrest", [128, B * S])
        qparts = sb("qparts", [128, 3, B * S], BF16)
        qpair = sb("qpair", [128, 3, B, 2, S], BF16)
        parity = sb("parity", [128, 2])
        ident = sb("ident", [128, 128])
        identb = sb("identb", [128, 128], BF16)
        ones_rows = sb("ones_rows", [MROWS, KEYS // 2])
        cols = sb("cols", [128, 5])
        abq_s = sb("abq_s", [128, 1])
        rows = sb("rows", [128, 4, D])
        out_bias = sb("out_bias", [128, D])
        wq_sb, wk_sb, wv_sb, wo_sb = (sb(n, [128, D]) for n in ("wq_sb", "wk_sb", "wv_sb", "wo_sb"))
        aq_sb, ak_sb, av_sb = (sb(n, [128, D]) for n in ("aq_sb", "ak_sb", "av_sb"))
        ctx_sb = sb("ctx_sb", [128, KT, D])
        ctxT = sb("ctxT", [128, KEYS])
        kparts = sb("kparts", [128, 3, KEYS], BF16)
        krest = sb("krest", [128, 2, 512])
        kstack = sb("kstack", [128, 2, PAIRS, KEYS], BF16)
        qstack = sb("qstack", [128, B, PAIRS, 2 * S], BF16)
        vt = sb("vt", [128, 2, KT, H, DK + 1])
        smax = sb("smax", [128, 2, 2, CHUNKS])
        negmax = sb("negmax", [128, 2, 2])
        mrest = sb("mrest", [128, 2, 2])
        mparts = sb("mparts", [128, 2, 2, MROWS], BF16)
        probs = sb("probs", [128, 4, 512])
        oT = sb("oT", [128, 2, S])
        osum = sb("osum", [128, 2, PAIRS, 2, DK + 1])
        rsum = sb("rsum", [128, 2, PAIRS, 2])
        att = sb("att", [128, D])
        attT = sb("attT", [128, S])
        x1 = sb("x1", [128, D])
        x1v = sb("x1v", [128, D])
        t_stats = sb("t_stats", [128, 6])
        t_mom = sb("t_mom", [128, 2])
        t_rstd = sb("t_rstd", [128, 1])
        t_xn = sb("t_xn", [128, D])
        t_xnT = sb("t_xnT", [128, S])
        s_qT = sb("s_qT", [128, S])
        s_kT = sb("s_kT", [128, S])
        s_v = sb("s_v", [128, D])
        s_negmax = sb("s_negmax", [128, 1])
        s_sum = sb("s_sum", [128, 1])
        s_rsum = sb("s_rsum", [128, 1])
        s_p = sb("s_p", [128, S])
        s_pT = sb("s_pT", [128, S])
        x2 = sb("x2", [128, B, D])
        x2b = sb("x2b", [128, B, D])
        f_xnT = sb("f_xnT", [128, B * S])
        f_h = probs
        stage_w = sb("stage_w", [128, 2, 2 * HID])
        up_y = sb("up_y", [128, 2, HID])
        row_y = sb("row_y", [1, 2, HID])
        BLOCK = 32
        BLOCKS, INNER = HID // BLOCK, BLOCK.bit_length() - 1
        block_y = sb("block_y", [BLOCKS, 2, BLOCK])
        block_w = sb("block_w", [BLOCKS, INNER, 2 * BLOCK])
        down_y = sb("down_y", [128, 2, HID])
        bf_a, bf_b = qf, qrest
        ub_row = sb("ub_row", [1, HID])
        up_b = row_y[:, 0, :]
        up_bcol = sb("up_bcol", [128, HB])
        w_dn = xnT[:].rearrange("p (j d) -> p j d", j=HB)
        y_sb = xn
        mask_min = sb("mask_min", [128, B])
        mask_low = sb("mask_low", [128, 1])
        flag_f = sb("flag_f", [1, 1])
        flag = sb("flag", [1, 1], I32)
        mask_sb = kstack[:, 0, :, :].rearrange("p a k -> p (a k)").bitcast(I32).rearrange("p (b k) -> p b k", b=B)
        g_mem = kstack[:].rearrange("p a b k -> p (a b k)").bitcast(F32)
        g_kT, g_keep, g_drop, g_s, g_pT, g_v, g_mask = (g_mem[:, KEYS * i:KEYS * i + KEYS] for i in range(7))
        g_q, g_qh, g_heads, g_negmax, g_sum = (g_mem[:, a:b] for a, b in (
            (14336, 14848), (14848, 14976), (14976, 14992), (14992, 14993), (14993, 14994)))

        ps_a = psum("ps_a", [128, 2, 512])
        ps_b = psum("ps_b", [128, 3, 512])
        ps_o = psum("ps_o", [128, 2, 512])
        ps_m = psum("ps_m", [128, 512])

        in_x, in_x1, in_wq, in_wk, in_wv, in_rows, in_tail = map(sem, ("in_x", "in_x1", "in_wq", "in_wk", "in_wv", "in_rows", "in_tail"))
        in_ctx = [sem(f"in_ctx{c}") for c in range(CHUNKS)]
        in_ffn, in_row, row_out = sem("in_ffn"), sem("in_row"), sem("row_out")
        in_stage = [sem("in_stage0"), sem("in_stage1")]
        q_out0, q_out = sem("q_out0"), sem("q_out")
        q_in = [sem(f"q_in{b}") for b in range(B)]
        k_in = [sem(f"k_in{p}") for p in range(PAIRS)]
        k_in_pool = [sem("k_in_pool0"), sem("k_in_pool1")]
        ones_in = sem("ones_in")
        y_out = sem("y_out")
        dve = sem("dve_chain")
        pool = sem("pool_chain")
        act = sem("act_chain")
        consts = sem("consts")
        var_ready, rstd_ready, xn_ready, xnT_ps, xnT_ready, q_ps, qpair_ready = map(
            sem, ("var_ready", "rstd_ready", "xn_ready", "xnT_ps", "xnT_ready", "q_ps", "qpair_ready"))
        ctxT_ps, ctxT_ready, k_ps, k1_ready, k2_ready, k3_ready, v_ps, v_ready = map(
            sem, ("ctxT_ps", "ctxT_ready", "k_ps", "k1_ready", "k2_ready", "k3_ready", "v_ps", "v_ready"))
        a_ps, a_max, b_ps, p_ready, pv_done = map(sem, ("a_ps", "a_max", "b_ps", "p_ready", "pv_done"))
        negmax_ready, mparts_ready, m_ps, m_ready = map(sem, ("negmax_ready", "mparts_ready", "m_ps", "m_ready"))
        oT_ready, o_ps, osum_ready, att_ready, o_clear = map(sem, ("oT_ready", "o_ps", "osum_ready", "att_ready", "o_clear"))
        tail_ps, tail_sb, t_var, t_rs, t_xn_ready, s_max_ready, row_sums = map(
            sem, ("tail_ps", "tail_sb", "t_var", "t_rs", "t_xn_ready", "s_max_ready", "row_sums"))
        up_ready, up_b_ready, down_ready, up_ps, up_bps, up_bcol_ready, gelu_ready, dn_tps, w_dn_ready, dn_ps, y_ready = map(
            sem, ("up_ready", "up_b_ready", "down_ready", "up_ps", "up_bps", "up_bcol_ready", "gelu_ready",
                  "dn_tps", "w_dn_ready", "dn_ps", "y_ready"))

        mask_in = sem("mask_in")
        mask_read, low_ready, low_ps, low_read, flag_ready = map(
            sem, ("mask_read", "low_ready", "low_ps", "low_read", "flag_ready"))
        q_saved, g_in_q, g_in_mask, g_mask_read, g_k_ready, g_qh_ready, g_s_ps, g_max_ready, g_p_ready = map(
            sem, ("q_saved", "g_in_q", "g_in_mask", "g_mask_read", "g_k_ready", "g_qh_ready", "g_s_ps", "g_max_ready", "g_p_ready"))
        g_pT_ps, g_pT_ready, g_o_ps, g_o_read, g_dve = map(
            sem, ("g_pT_ps", "g_pT_ready", "g_o_ps", "g_o_read", "g_dve"))

        def chain_of(eng, s):
            n = [0]

            def link(ins, wait=True):
                n[0] += 1
                ins.then_inc(s, 1)
                if wait:
                    eng.wait_ge(s, n[0])
            return link

        LAG = 2
        AHEAD = 2
        PREP = [(what, c) for c in range(CHUNKS) for what in ("turn", "k")] + [("v", c) for c in range(CHUNKS)]
        PREP_AT = {0: ("turn", 0), 2: ("turn", 1), 4: ("v", 0), 6: ("v", 1), 8: ("turn", 2), 14: ("turn", 3),
                   48: ("v", 2), 50: ("v", 3), 22: ("k", 0), 26: ("k", 1), 30: ("k", 2), 34: ("k", 3)}
        EARLY = {2: ("turn", 0), 3: ("turn", 1), 4: ("turn", 2), 5: ("turn", 3), 8: ("v", 0), 9: ("v", 1)}
        PREP_FIRST = {0: ("v", 2), 4: ("v", 3), 22: ("k", 0), 26: ("k", 1), 30: ("k", 2), 34: ("k", 3)}
        TAIL = ["turn_att", "project", "turn_x1", "qkv", "scores", "turn_p", "self_out", "turn_x2"]
        TAIL_AT = dict(zip((10, 12, 20, 38, 41, 44, 46, 54), TAIL))
        FFN_AT = {50: ("ffn", 0, "bias", 0), 52: ("ffn", 0, "down", 0)}

        def misc_task(g, k):
            b, p = divmod(g, PAIRS)
            at = STEPS * p + k
            prep_at = PREP_AT if b else PREP_FIRST
            if b + 1 < B and at in prep_at:
                return ("prep", b + 1) + prep_at[at]
            if b > 0 and at in TAIL_AT:
                return "tail", b - 1, TAIL_AT[at], 0
            if b == B - 1:
                return FFN_AT.get(at)
            return None

        SEARCH_AT = (48, 53, 57, 60)

        def ahead(g, k):
            if g == 0:
                return [(AHEAD - 1) * STEPS + 2 * k, (AHEAD - 1) * STEPS + 2 * k + 1]
            return [STEPS * (g + AHEAD) + k] if g + AHEAD < G else []

        def at(g, k, step):
            return STEPS * (g % PAIRS) + k == step

        def read_of(task):
            kind, b, what, c = task
            if kind == "ffn":
                return (up_bcol_ready if what == "bias" else w_dn_ready), 1
            if kind == "prep":
                if what == "k" and b >= B:
                    return g_k_ready, CHUNKS * (b - B) + c + 1
                return {"turn": ctxT_ready, "k": k2_ready, "v": v_ready}[what], CHUNKS * b + c + 1
            return tail_sb, len(TAIL) * b + TAIL.index(what) + 1

        MISC = (ps_m[:], ps_b[:, 2, :])
        bank, before = {}, {}
        last = [(v_ready, CHUNKS), (v_ready, CHUNKS)]
        for t_ in ([("prep", 1) + early_ for early_ in EARLY.values()]
                   + [misc_task(g_, k_) for g_ in range(G) for k_ in range(STEPS)]):
            if t_:
                bank[t_] = len(bank) % 2
                before[t_] = last[bank[t_]]
                last[bank[t_]] = read_of(t_)
        second_free = last[1]
        for t_ in ([("tail", B - 1, what_, 0) for what_ in TAIL]
                   + [t_ for b_ in range(B, 2 * B) for t_ in [("prep", b_) + prep_ for prep_ in PREP]
                      + [("tail", b_, what_, 0) for what_ in TAIL]]):
            bank[t_] = 0
            before[t_] = last[0] if t_[:3] != ("prep", B, PREP[0][0]) or t_[3] != PREP[0][1] else (y_ready, B)
            last[0] = read_of(t_)

        PHASES = ((0, 1), (1, B))
        WARM, KEEP = 16, 8
        K_BANK = (ps_a[:, 0, :], ps_a[:, 1, :], ps_o[:, 1, :], ps_b[:, 1, :])
        V_BANK = (ps_m[:], ps_b[:, 0, :], ps_b[:, 2, :], ps_m[:])

        def k_loaded(b, p):
            if p < PAIRS - 2:
                return k_in[p], 16 * SLOTS * (b + 1)
            return (k_in[p], 16 * SLOTS * b) if b else (k_in_pool[p - PAIRS + 2], 16 * SLOTS)

        FFN_PHASES = ((0, B - 1), (B - 1, B))
        DOWN_BANK = (ps_o[:, 0, :], ps_o[:, 1, :], ps_a[:, 1, :], ps_m[:])

        def up_bank(j):
            return ps_b[:, j, :] if j < 3 else ps_a[:, 0, :]

        def g_bank(c):
            return ps_a[:, c, :] if c < 2 else ps_b[:, c - 2, :]

        def masked(eng):
            eng.wait_ge(flag_ready, 1)
            return eng.If(eng.value_load(flag[:], min_val=0, max_val=1) == 1)

        block = es.enter_context(nc.Block())

        @block.sync
        def _(sp):
            sp.dma_start(x_sb[:, 0, :], x[0]).then_inc(in_x, 16)
            sp.dma_start(ctx_sb[:, 0:4, :], ctx[0, 0:512, :].rearrange("(t k) d -> k t d", k=128)).then_inc(in_ctx[0], 16)
            sp.dma_start(wq_sb[:], w_q).then_inc(in_wq, 16)
            sp.dma_start(x_sb[:, 1:B, :], x[1:B].rearrange("b s d -> s b d")).then_inc(in_x1, 16)
            sp.dma_start(wk_sb[:], w_k).then_inc(in_wk, 16)
            sp.dma_start(cols[:], bias_cols).then_inc(in_wk, 16)
            for c in range(1, CHUNKS):
                sp.dma_start(ctx_sb[:, 4 * c:4 * c + 4, :],
                             ctx[0, 512 * c:512 * c + 512, :].rearrange("(t k) d -> k t d", k=128)).then_inc(in_ctx[c], 16)
            sp.dma_start(wv_sb[:], w_v).then_inc(in_wv, 16)
            sp.wait_ge(consts, 3)
            for buf in range(2):
                sp.dma_start(kstack[ROWS:ROWS + MROWS, buf, :, :].bitcast(F32),
                             ones_rows[:].unsqueeze(1).broadcast_to([MROWS, PAIRS, KEYS // 2])).then_inc(ones_in, 16)

            def load_q(b):
                for s in range(SLOTS):
                    sp.dma_start(qstack[16 * s:16 * s + 16, b, :, :],
                                 q_scratch[:, Q_PART[s], b, :].rearrange("(p r) c -> r p c", r=16)).then_inc(q_in[b], 16)

            def load_k(b, p, slots=range(SLOTS)):
                for s in slots:
                    sp.dma_start(kstack[16 * s:16 * s + 16, b % 2, p, :],
                                 kparts[16 * p:16 * p + 16, K_PART[s], :]).then_inc(k_in[p], 16)

            def load_ctx(b, c):
                sp.wait_ge(ctxT_ps, CHUNKS * (b - 1) + c + 1)
                sp.dma_start(ctx_sb[:, 4 * c:4 * c + 4, :],
                             ctx[b % B, 512 * c:512 * c + 512, :].rearrange("(t k) d -> k t d", k=128)).then_inc(in_ctx[c], 16)

            sp.wait_ge(qpair_ready, 2)
            sp.dma_start(q_scratch[:, :, 0, :], qpair[:, :, 0, :, :].rearrange("p i h s -> p i (h s)")).then_inc(q_out0, 16)
            sp.wait_ge(q_out0, 16)
            load_q(0)
            sp.wait_ge(k1_ready, CHUNKS)
            load_k(0, 0, range(0, 3))
            sp.wait_ge(k2_ready, CHUNKS)
            load_k(0, 0, range(3, 5))
            sp.wait_ge(k3_ready, CHUNKS)
            load_k(0, 0, range(5, 6))
            for c in range(CHUNKS):
                load_ctx(1, c)
            load_k(0, 1)
            load_k(0, 2)
            sp.dma_start(rows[:].rearrange("p r d -> p (r d)"), bias_rows.partition_broadcast(128)).then_inc(in_rows, 16)
            sp.wait_ge(qpair_ready, 4)
            sp.dma_start(q_scratch[:, :, 1:B, :], qpair[:, :, 1:B, :, :].rearrange("p i b h s -> p i b (h s)")).then_inc(q_out, 16)
            sp.dma_start(q_full, qf[:]).then_inc(q_saved, 16)
            for p in range(3, PAIRS - 2):
                load_k(0, p)
            sp.wait_ge(q_out, 16)
            for b in range(1, B):
                load_q(b)
            for dst, src in ((wo_sb, w_o), (aq_sb, a_wqT), (ak_sb, a_wkT), (av_sb, a_wvT)):
                sp.dma_start(dst[:], src).then_inc(in_tail, 16)
            for b in range(1, B):
                if b + 1 < B:
                    for c in range(CHUNKS):
                        load_ctx(b + 1, c)
                sp.wait_ge(k3_ready, CHUNKS * (b + 1))
                for p in range(PAIRS):
                    if b >= 2:
                        sp.wait_ge(b_ps, STEPS * ((b - 2) * PAIRS + p + 1))
                    load_k(b, p)

            for b in range(B):
                sp.wait_ge(b_ps, STEPS * (PAIRS * (B - 1) + b))
                sp.dma_start(mask_sb[:, b, :], mask[b, 0]).then_inc(mask_in, 16)

            def store(turn):
                for b in range(B):
                    sp.wait_ge(y_ready, B * turn + b + 1)
                    sp.dma_start(out[b], y_sb[:, b, :]).then_inc(y_out, 16)
                sp.wait_ge(y_out, 16 * B * (turn + 1))

            store(0)
            with masked(sp):
                sp.dma_start(g_q, q_full).then_inc(g_in_q, 16)
                for b in range(B):
                    for c in range(CHUNKS):
                        load_ctx(B + b, c)
                    if b >= 1:
                        sp.wait_ge(g_mask_read, b)
                    sp.dma_start(g_mask.bitcast(I32), mask[b, 0]).then_inc(g_in_mask, 16)
                store(1)

        @block.gpsimd
        def _(gp):
            link = chain_of(gp, pool)
            link(nc.gpsimd.memset(ident[:], 0.0))
            link(nc.gpsimd.affine_select(out=ident[:], in_=ident[:], compare_op=ALU.not_equal, fill=1.0, base=0,
                                         pattern=[[-1, 128]], channel_multiplier=1))
            nc.gpsimd.tensor_copy(identb[:], ident[:]).then_inc(consts, 1)
            nc.gpsimd.memset(neg_half[:], -0.5).then_inc(consts, 1)
            nc.gpsimd.memset(ones_rows[:], 1.0019378662109375).then_inc(consts, 1)
            gp.wait_ge(consts, 3)
            for i, (b0, b1) in enumerate(PHASES):
                gp.wait_ge(var_ready, i + 1)
                nc.gpsimd.tensor_tensor(rstd[:, b0:b1], moments[:, b0:b1, 1], neg_half[:, b0:b1],
                                        ALU.pow).then_inc(rstd_ready, 1)
            link(nc.gpsimd.memset(vt[:, :, :, :, DK:DK + 1], 1.0))
            def split_third(b, c):
                n = CHUNKS * b + c
                gp.wait_ge(k2_ready, n + 1)
                sl = slice(512 * c, 512 * c + 512)
                nc.gpsimd.tensor_tensor(kparts[:, 2, sl], krest[:, c % 2, :], kparts[:, 1, sl],
                                        ALU.subtract).then_inc(k3_ready, 1)

            def split_max(g):
                i = g % 2
                gp.wait_ge(negmax_ready, g + 1)
                if g >= 2:
                    gp.wait_ge(m_ps, g - 1)
                link(nc.gpsimd.tensor_copy(mparts[:, i, :, 0], negmax[:, i, :]))
                link(nc.gpsimd.tensor_tensor(mrest[:, i, :], negmax[:, i, :], mparts[:, i, :, 0], ALU.subtract))
                link(nc.gpsimd.tensor_copy(mparts[:, i, :, 1], mrest[:, i, :]))
                nc.gpsimd.tensor_tensor(mparts[:, i, :, 2], mrest[:, i, :], mparts[:, i, :, 1],
                                        ALU.subtract).then_inc(mparts_ready, 1)

            def load_stage(n):
                src = w_up[n] if n < STAGES else w_down[2 * STAGES - 1 - n]
                gp.dma_start(stage_w[:, n % 2, :], src.partition_broadcast(128)).then_inc(in_stage[n % 2], 16)

            def butterfly(n, y, w):
                s = 2 ** (n if n < STAGES else 2 * STAGES - 1 - n)
                parts, _, size = y.shape
                w = w.rearrange("p (n s i j) -> p n i j s", s=s, i=2, j=2)
                yr = y[:, n % 2, :].rearrange("p (n i s) -> p n i s", i=2, s=s)
                shape = [parts, size // (2 * s), 2, s]
                first, second = (yr[:, :, e:e + 1, :].broadcast_to(shape) for e in range(2))
                w0, w1 = (w[:, :, :, e, :] if n < STAGES else w[:, :, e, :, :] for e in range(2))
                a, b = bf_a[0:parts, 0:size], bf_b[0:parts, 0:size]
                va, vb = (t.rearrange("p (n i s) -> p n i s", i=2, s=s) for t in (a, b))
                link(nc.gpsimd.tensor_tensor(va, w0, first, ALU.mult), wait=False)
                link(nc.gpsimd.tensor_tensor(vb, w1, second, ALU.mult))
                link(nc.gpsimd.tensor_tensor(y[:, (n + 1) % 2, :], a, b, ALU.add))

            def stage_part(part):
                what, n = part
                if what == "blocks":
                    gp.wait_ge(in_ffn, 80)
                    gp.wait_ge(q_saved, 16)
                    for i in range(INNER):
                        butterfly(i, block_y, block_w[:, i, :])
                    gp.dma_start(row_scratch.rearrange("o (p c) -> (o p) c", p=BLOCKS),
                                 block_y[:, INNER % 2, :]).then_inc(row_out, 16)
                    return
                if n == 1:
                    gp.wait_ge(row_out, 16)
                    gp.dma_start(row_y[:, INNER % 2, :], row_scratch).then_inc(in_row, 16)
                if what == "row":
                    if n == INNER:
                        gp.wait_ge(in_row, 16)
                    butterfly(n, row_y, stage_w[0:1, n % 2, :])
                    if n == STAGES - 1:
                        nc.gpsimd.tensor_tensor(up_b, row_y[:, STAGES % 2, :], ub_row[:], ALU.add).then_inc(up_b_ready, 1)
                else:
                    gp.wait_ge(in_stage[n % 2], 16 * (n // 2 + 1))
                    butterfly(n, up_y if n < STAGES else down_y, stage_w[:, n % 2, :])
                if n + 2 < 2 * STAGES and not (what == "up" and INNER <= n):
                    load_stage(n + 2)
                if n == 2 * STAGES - 1:
                    gp.wait_ge(in_rows, 16)
                    nc.gpsimd.tensor_tensor(out_bias[:], rows[:, 2, :], rows[:, 3, :], ALU.add).then_inc(down_ready, 1)

            PARTS = [("blocks", 0)] + [("up", n) for n in range(INNER)]
            for n in range(INNER, STAGES):
                PARTS += [("up", n), ("row", n)]
            PARTS += [("down", n) for n in range(STAGES, 2 * STAGES)]

            def power(i):
                gp.wait_ge(t_var, i + 1)
                nc.gpsimd.tensor_tensor(t_rstd[:], t_mom[:, 1:2], neg_half[:, 0:1], ALU.pow).then_inc(t_rs, 1)

            def load_k(p):
                for s in range(SLOTS):
                    gp.dma_start(kstack[16 * s:16 * s + 16, 0, p, :],
                                 kparts[16 * p:16 * p + 16, K_PART[s], :]).then_inc(k_in_pool[p - PAIRS + 2], 16)

            for c in range(CHUNKS):
                split_third(0, c)
            gp.wait_ge(k3_ready, CHUNKS)
            load_k(PAIRS - 1)
            split_max(0)
            load_k(PAIRS - 2)
            part = 0
            for g in range(G):
                b, p = divmod(g, PAIRS)
                if g + 1 < G:
                    split_max(g + 1)
                if g == 0:
                    gp.dma_start(up_y[:, 0, :], w_exp).then_inc(in_ffn, 16)
                    gp.dma_start(down_y[:, STAGES % 2, :], w_conT).then_inc(in_ffn, 16)
                    gp.dma_start(block_y[:, 0, :], b_exp.rearrange("o (p c) -> (o p) c", p=BLOCKS)).then_inc(in_ffn, 16)
                    gp.dma_start(block_w[:], w_up[0:INNER, :].rearrange("s (p c) -> p s c", p=BLOCKS)).then_inc(in_ffn, 16)
                    gp.dma_start(ub_row[:], up_bias).then_inc(in_ffn, 16)
                    load_stage(0)
                    load_stage(1)
                if b > 0 and p == 6:
                    power(2 * (b - 1) + 1)
                if b + 1 < B and p in (3, 4):
                    split_third(b + 1, 2 * (p - 3))
                    split_third(b + 1, 2 * (p - 3) + 1)
                elif g >= 1 and part < len(PARTS):
                    stage_part(PARTS[part])
                    part += 1
                if b > 0 and p == 1:
                    power(2 * (b - 1))
            power(2 * (B - 1))
            power(2 * (B - 1) + 1)
            with masked(gp):
                for b in range(B, 2 * B):
                    power(2 * b)
                    power(2 * b + 1)

        @block.scalar
        def _(act_e):
            link = chain_of(act_e, act)

            def take(task, src):
                kind, b, what, c = task
                n = CHUNKS * b + c
                sl = slice(512 * c, 512 * c + 512)
                if what == "turn":
                    act_e.wait_ge(ctxT_ps, n + 1)
                    nc.scalar.copy(ctxT[:, sl], src).then_inc(ctxT_ready, 1)
                elif what == "k" and b >= B:
                    act_e.wait_ge(k_ps, n + 1)
                    nc.scalar.activation(g_kT[:, sl], src, ACT.Identity, bias=cols[:, 1:2]).then_inc(g_k_ready, 1)
                elif what == "v" and b >= B:
                    act_e.wait_ge(v_ps, n + 1)
                    nc.scalar.copy(g_v[:, sl], src).then_inc(v_ready, 1)
                elif kind == "ffn":
                    return
                elif what == "k":
                    act_e.wait_ge(k_ps, n + 1)
                    if b == 0:
                        act_e.wait_ge(in_wk, 32)
                    elif c == 0:
                        for p in range(PAIRS):
                            act_e.wait_ge(*k_loaded(b - 1, p))
                    nc.scalar.activation(kparts[:, 0, sl], src, ACT.Identity, bias=cols[:, 1:2]).then_inc(k1_ready, 1)
                elif what == "v":
                    act_e.wait_ge(v_ps, n + 1)
                    if b >= 2:
                        act_e.wait_ge(pv_done, STEPS * PAIRS * (b - 1))
                    nc.scalar.copy(vt[:, b % 2, 4 * c:4 * c + 4, :, 0:DK],
                                   src.rearrange("p (t h d) -> p t h d", t=4, h=H)).then_inc(v_ready, 1)
                else:
                    if what in ("project", "self_out"):
                        return
                    act_e.wait_ge(tail_ps, len(TAIL) * b + TAIL.index(what) + 1)
                    if what == "turn_att":
                        nc.scalar.activation(attT[:], src[:, 0:S], ACT.Identity, bias=cols[:, 2:3]).then_inc(tail_sb, 1)
                    elif what == "turn_x1":
                        nc.scalar.copy(t_xnT[:], src[:, 0:S]).then_inc(tail_sb, 1)
                    elif what == "qkv":
                        link(nc.scalar.activation(s_qT[:], src[:, 0:S], ACT.Identity, bias=abq_s[:], scale=float(D) ** -0.5), wait=False)
                        link(nc.scalar.activation(s_kT[:], src[:, S:2 * S], ACT.Identity, bias=cols[:, 4:5]), wait=False)
                        nc.scalar.copy(s_v[:], src[:, 2 * S:2 * S + D]).then_inc(tail_sb, 1)
                    elif what == "scores":
                        act_e.wait_ge(s_max_ready, b + 1)
                        nc.scalar.activation(s_p[:], src[:, 0:S], ACT.Exp, bias=s_negmax[:],
                                             accum_out=s_sum[:]).then_inc(tail_sb, 1)
                    elif what == "turn_p":
                        nc.scalar.copy(s_pT[:], src[:, 0:S]).then_inc(tail_sb, 1)
                    elif what == "turn_x2":
                        nc.scalar.copy(f_xnT[:, S * (b % B):S * (b % B) + S], src[:, 0:S]).then_inc(tail_sb, 1)

            def exp_step(u):
                act_e.wait_ge(b_ps, u + 1)
                if u >= 4:
                    act_e.wait_ge(pv_done, u - 3)
                nc.scalar.activation(probs[:, u % 4, :], ps_b[:, u % 2, :], ACT.Exp).then_inc(p_ready, 1)

            def take_outputs(g):
                act_e.wait_ge(pv_done, STEPS * (g + 1))
                if g >= 2:
                    act_e.wait_ge(o_ps, g - 1)
                nc.scalar.copy(oT[:, g % 2, :], ps_o[:, g % 2, 0:S]).then_inc(oT_ready, 1)

            def place_max(g):
                act_e.wait_ge(m_ps, g + 1)
                nc.scalar.copy(qstack[ROWS:ROWS + MROWS, g // PAIRS, g % PAIRS, :],
                               ps_o[ROWS:ROWS + MROWS, g % 2, 256:384].bitcast(BF16)).then_inc(m_ready, 1)

            def take_xn(i):
                b0, b1 = PHASES[i]
                act_e.wait_ge(xnT_ps, i + 1)
                nc.scalar.copy(xnT[:, S * b0:S * b1], ps_m[:, S * b0:S * b1]).then_inc(xnT_ready, 1)

            take(("prep", 0, "turn", 0), ps_b[:, 0, :])
            take_xn(0)
            for c in range(CHUNKS):
                if c + 1 < CHUNKS:
                    take(("prep", 0, "turn", c + 1), ps_b[:, (c + 1) % 3, :])
                take(("prep", 0, "k", c), K_BANK[c])
                if c == 2:
                    take_xn(1)
            link(nc.scalar.mul(abq_s[:], cols[:, 3:4], float(D) ** -0.5))
            for c in range(CHUNKS):
                take(("prep", 0, "v", c), V_BANK[c])
            for early in EARLY.values():
                take(("prep", 1) + early, MISC[bank[("prep", 1) + early]])
            place_max(0)
            for g in range(G):
                for k in range(STEPS):
                    exp_step(STEPS * g + k)
                    if k == 2 and g >= 1:
                        take_outputs(g - 1)
                    if k == 6 and g + 1 < G:
                        place_max(g + 1)
                    g_, k_ = divmod(STEPS * g + k - 1, STEPS)
                    if g_ >= 0 and misc_task(g_, k_):
                        take(misc_task(g_, k_), MISC[bank[misc_task(g_, k_)]])
            take_outputs(G - 1)

            def tail(b):
                for what in TAIL:
                    take(("tail", b, what, 0), ps_m[:])

            def hidden(turn, i):
                b0, b1 = FFN_PHASES[i]
                sl = slice(S * b0, S * b1)
                act_e.wait_ge(up_bcol_ready, 1)
                for j in range(HB):
                    act_e.wait_ge(up_ps, HB * (2 * turn + i) + j + 1)
                    nc.scalar.activation(f_h[:, j, sl], up_bank(j)[:, sl], ACT.Gelu,
                                         bias=up_bcol[:, j:j + 1]).then_inc(gelu_ready, 1)

            def last_tail(turn):
                for what in TAIL:
                    if what == "self_out":
                        hidden(turn, 0)
                    take(("tail", B * turn + B - 1, what, 0), ps_m[:])
                hidden(turn, 1)

            last_tail(0)
            with masked(act_e):
                act_e.wait_ge(y_out, 16 * B)
                for b in range(B):
                    for what, c in PREP:
                        take(("prep", B + b, what, c), ps_m[:])
                    with act_e.Fori(0, H) as h:
                        n = h + H * b + 1
                        act_e.wait_ge(g_max_ready, n)
                        nc.scalar.activation(g_s, g_s, ACT.Exp, bias=g_negmax, accum_out=g_sum).then_inc(g_p_ready, 1)
                        act_e.wait_ge(g_pT_ps, n)
                        for c in range(CHUNKS):
                            ins = nc.scalar.copy(g_pT[:, 512 * c:512 * c + 512], g_bank(c))
                        ins.then_inc(g_pT_ready, 1)
                    if b < B - 1:
                        tail(B + b)
                last_tail(1)

        @block.vector
        def _(ve):
            link = chain_of(ve, dve)

            def norm_stats(src, st, mom, done):
                link(nc.vector.bn_stats(st, src))
                link(nc.vector.bn_aggr(mom, st))
                nc.vector.tensor_scalar_add(mom[:, 1:2], mom[:, 1:2], EPS).then_inc(done, 1)

            def split_k(b, c, src):
                n = CHUNKS * b + c
                sl = slice(512 * c, 512 * c + 512)
                ve.wait_ge(k1_ready, n + 1)
                if n >= 2:
                    ve.wait_ge(k3_ready, n - 1)
                link(nc.vector.scalar_tensor_tensor(out=krest[:, c % 2, :], in0=src, scalar=cols[:, 1:2],
                                                    in1=kparts[:, 0, sl], op0=ALU.add, op1=ALU.subtract))
                nc.vector.tensor_copy(kparts[:, 1, sl], krest[:, c % 2, :]).then_inc(k2_ready, 1)

            def chunk_max(ua):
                g, k = divmod(ua, STEPS)
                ve.wait_ge(a_ps, ua + 1)
                nc.vector.tensor_reduce(smax[:, g % 2, k // CHUNKS, k % CHUNKS:k % CHUNKS + 1], ps_a[:, ua % 2, :],
                                        AX.X, ALU.max).then_inc(a_max, 1)

            def row_max(g):
                ve.wait_ge(a_max, STEPS * (g + 1))
                if g >= 2:
                    ve.wait_ge(mparts_ready, g - 1)
                nc.vector.tensor_reduce(negmax[:, g % 2, :], smax[:, g % 2, :, :], AX.X, ALU.max,
                                        negate=True).then_inc(negmax_ready, 1)

            def sum_outputs(g):
                ve.wait_ge(o_ps, g + 1)
                src = ps_o[:, g % 2, 128:256].rearrange("q (e h r) -> q h r e", e=2, h=2)[:, :, 0:DK + 1, :]
                nc.vector.tensor_reduce(osum[:, (g // PAIRS) % 2, g % PAIRS, :, :], src, AX.X, ALU.add).then_inc(osum_ready, 1)

            def normalise(b):
                if b < B:
                    ve.wait_ge(osum_ready, PAIRS * (b + 1))
                if b >= 1:
                    ve.wait_ge(tail_ps, len(TAIL) * (b - 1) + 1)
                i = b % 2
                link(nc.vector.reciprocal(rsum[:, i, :, :], osum[:, i, :, :, DK]))
                nc.vector.tensor_tensor(att[:].rearrange("q (p h d) -> q p h d", p=PAIRS, h=2), osum[:, i, :, :, 0:DK],
                                        rsum[:, i, :, :].unsqueeze(3).broadcast_to([128, PAIRS, 2, DK]),
                                        ALU.mult).then_inc(att_ready, 1)

            def take(task, src):
                kind, b, what, c = task
                if what == "k" and b < B:
                    split_k(b, c, src)
                    return
                if kind == "ffn":
                    if what == "bias":
                        ve.wait_ge(up_bps, 1)
                        nc.vector.tensor_copy(up_bcol[:], src[:, 0:HB]).then_inc(up_bcol_ready, 1)
                    else:
                        ve.wait_ge(dn_tps, 1)
                        nc.vector.tensor_copy(xnT[:], src).then_inc(w_dn_ready, 1)
                    return
                if kind == "prep" or what not in ("project", "scores", "self_out"):
                    return
                if what == "self_out":
                    ve.wait_ge(tail_sb, len(TAIL) * b + TAIL.index("scores") + 1)
                    link(nc.vector.reciprocal(s_rsum[:], s_sum[:]))
                ve.wait_ge(tail_ps, len(TAIL) * b + TAIL.index(what) + 1)
                if what == "project":
                    nc.vector.tensor_tensor(x1[:], src[:, 0:D], xo_sb[:, b % B, :], ALU.add).then_inc(tail_sb, 1)
                    ve.wait_ge(tail_sb, len(TAIL) * b + TAIL.index(what) + 1)
                    norm_stats(x1[:], t_stats[:], t_mom[:], t_var)
                    link(nc.vector.tensor_tensor(x1v[:], x1[:], rows[:, 1, :], ALU.add), wait=False)
                elif what == "scores":
                    nc.vector.tensor_reduce(s_negmax[:], src[:, 0:S], AX.X, ALU.max, negate=True).then_inc(s_max_ready, 1)
                elif what == "self_out":
                    nc.vector.scalar_tensor_tensor(out=x2[:, b % B, :], in0=src[:, 0:D], scalar=s_rsum[:], in1=x1v[:],
                                                   op0=ALU.mult, op1=ALU.add).then_inc(tail_sb, 1)
                    ve.wait_ge(tail_sb, len(TAIL) * b + TAIL.index(what) + 1)
                    norm_stats(x2[:, b % B, :], t_stats[:], t_mom[:], t_var)

            def tail_norm(b, second):
                ve.wait_ge(t_rs, 2 * b + second + 1)
                nc.vector.tensor_scalar(t_xn[:], x2[:, b % B, :] if second else x1[:], t_mom[:, 0:1], t_rstd[:],
                                        ALU.subtract, ALU.mult).then_inc(t_xn_ready, 1)

            def search_mask(b):
                ve.wait_ge(mask_in, 16 * B)
                nc.vector.tensor_reduce(mask_min[:, b:b + 1], mask_sb[:, b, :], AX.X, ALU.min,
                                        apply_absolute_value=True).then_inc(mask_read, 1)

            def lowest_mask():
                ve.wait_ge(mask_read, B)
                nc.vector.tensor_reduce(mask_low[:], mask_min[:], AX.X, ALU.min).then_inc(low_ready, 1)

            def set_flag():
                ve.wait_ge(low_ps, 1)
                nc.vector.tensor_reduce(flag_f[:], ps_o[0:1, 0, 0:128], AX.X, ALU.min).then_inc(low_read, 1)
                ve.wait_ge(low_read, 1)
                nc.vector.tensor_scalar(flag[:], flag_f[:], 0.0, None, ALU.is_equal).then_inc(flag_ready, 1)

            def split_q(i):
                b0, b1 = PHASES[i]
                sl = slice(S * b0, S * b1)
                ve.wait_ge(q_ps, i + 1)
                link(nc.vector.tensor_scalar(qf[:, sl], ps_o[:, 0, sl], cols[:, 0:1], float(DK) ** -0.5, ALU.add, ALU.mult))
                link(nc.vector.tensor_copy(qparts[:, 0, sl], qf[:, sl]))
                link(nc.vector.tensor_tensor(qrest[:, sl], qf[:, sl], qparts[:, 0, sl], ALU.subtract))
                link(nc.vector.tensor_copy(qparts[:, 1, sl], qrest[:, sl]))
                link(nc.vector.tensor_tensor(qparts[:, 2, sl], qrest[:, sl], qparts[:, 1, sl], ALU.subtract))
                for j in range(2):
                    nc.vector.tensor_scalar(qpair[:, :, b0:b1, j, :], qparts[:, :, sl].rearrange("p i (b s) -> p i b s", s=S),
                                            parity[:, j:j + 1], None, ALU.mult).then_inc(qpair_ready, 1)

            def norm_x(i):
                b0, b1 = PHASES[i]
                ve.wait_ge(rstd_ready, i + 1)
                for b in range(b0, b1):
                    nc.vector.tensor_scalar(xn[:, b, :], x_sb[:, b, :], moments[:, b, 0:1], rstd[:, b:b + 1],
                                            ALU.subtract, ALU.mult).then_inc(xn_ready, 1)

            def stats_x(i):
                b0, b1 = PHASES[i]
                ve.wait_ge((in_x, in_x1)[i], 16)
                for b in range(b0, b1):
                    link(nc.vector.bn_stats(stats[:, b, :], x_sb[:, b, :]), wait=(b == b1 - 1))
                for b in range(b0, b1):
                    link(nc.vector.bn_aggr(moments[:, b, :], stats[:, b, :]), wait=(b == b1 - 1))
                nc.vector.tensor_scalar_add(moments[:, b0:b1, 1], moments[:, b0:b1, 1], EPS).then_inc(var_ready, 1)

            stats_x(0)
            ve.wait_ge(consts, 1)
            link(nc.vector.tensor_reduce(parity[:], ident[:].rearrange("p (a j d) -> p j a d", j=2, d=DK), AX.XY, ALU.add),
                 wait=False)
            norm_x(0)
            stats_x(1)
            ve.wait_ge(in_wk, 32)
            split_q(0)
            norm_x(1)
            for c in range(CHUNKS):
                split_k(0, c, K_BANK[c])
            split_q(1)
            for i in range(2):
                nc.vector.memset(ps_o[:, i, 0:S], 0.0).then_inc(o_clear, 1)
            for ua in range((AHEAD - 1) * STEPS):
                chunk_max(ua)
            row_max(0)
            for g in range(G):
                b, p = divmod(g, PAIRS)
                for k in range(STEPS):
                    for ua in ahead(g, k):
                        chunk_max(ua)
                    if k == (3 if g == 0 else 0) and g + 1 < G:
                        row_max(g + 1)
                    if k == 0 and g >= 2:
                        sum_outputs(g - 2)
                    if (g, k) == (6, 2):
                        ve.wait_ge(in_rows, 16)
                        link(nc.vector.tensor_tensor(xo_sb[:], x_sb[:], rows[:, 0:1, :].broadcast_to([128, B, D]), ALU.add),
                             wait=False)
                    if k == 0 and b > 0 and p == 1:
                        normalise(b - 1)
                    if b == B - 1 and STEPS * p + k in SEARCH_AT:
                        search_mask(SEARCH_AT.index(STEPS * p + k))
                    if b > 0 and (at(g, k, 18) or at(g, k, 51)):
                        tail_norm(b - 1, at(g, k, 51))
                    for late in (1, 2):
                        g_, k_ = divmod(STEPS * g + k - late, STEPS)
                        task = misc_task(g_, k_) if g_ >= 0 else None
                        if task and (task[2] == "k") == (late == 2):
                            take(task, MISC[bank[task]])
            sum_outputs(G - 2)
            sum_outputs(G - 1)
            normalise(B - 1)

            def tail(b):
                for what in TAIL:
                    if what in ("turn_x1", "turn_x2"):
                        tail_norm(b, what == "turn_x2")
                    take(("tail", b, what, 0), ps_m[:])
                    if (b, what) == (B - 1, "project"):
                        lowest_mask()
                    if (b, what) == (B - 1, "qkv"):
                        set_flag()

            def result(turn):
                if turn == 0:
                    ve.wait_ge(down_ready, 1)
                link(nc.vector.tensor_tensor(x2b[:], x2[:], out_bias[:].unsqueeze(1).broadcast_to([128, B, D]), ALU.add))
                for b in range(B):
                    ve.wait_ge(dn_ps, B * turn + b + 1)
                    nc.vector.tensor_tensor(y_sb[:, b, :], DOWN_BANK[b][:, 0:D], x2b[:, b, :], ALU.add).then_inc(y_ready, 1)

            tail(B - 1)
            result(0)
            with masked(ve):
                ve.wait_ge(y_out, 16 * B)
                link(nc.vector.tensor_reduce(g_heads, ident[:].rearrange("p (h d) -> p h d", d=DK), AX.X, ALU.add))
                ve.wait_ge(g_in_q, 16)
                for b in range(B):
                    ve.wait_ge(g_in_mask, 16 * (b + 1))
                    nc.vector.tensor_scalar(g_drop, g_mask.bitcast(I32), 0.0, None, ALU.is_equal).then_inc(g_mask_read, 1)
                    ve.wait_ge(g_mask_read, b + 1)
                    link(nc.vector.tensor_scalar(g_keep, g_drop, -1.0, 1.0, ALU.mult, ALU.add))
                    LINKS = 2 * CHUNKS
                    with ve.Fori(0, H) as h:
                        n = h + H * b + 1
                        nc.vector.tensor_scalar(g_qh, g_q[:, S * b:S * b + S], g_heads[:, bass.ds(h, 1)], None,
                                                ALU.mult).then_inc(g_qh_ready, 1)
                        ve.wait_ge(g_s_ps, n)
                        for c in range(CHUNKS):
                            sl = slice(512 * c, 512 * c + 512)
                            nc.vector.tensor_tensor(g_s[:, sl], g_bank(c), g_keep[:, sl], ALU.mult).then_inc(g_dve, 1)
                            ve.wait_ge(g_dve, (n - 1) * LINKS + 2 * c + 1)
                            nc.vector.scalar_tensor_tensor(out=g_s[:, sl], in0=g_drop[:, sl], scalar=-1e9, in1=g_s[:, sl],
                                                           op0=ALU.mult, op1=ALU.add).then_inc(g_dve, 1)
                        ve.wait_ge(g_dve, n * LINKS)
                        nc.vector.tensor_reduce(g_negmax, g_s, AX.X, ALU.max, negate=True).then_inc(g_max_ready, 1)
                        ve.wait_ge(g_o_ps, n)
                        sums = osum[:, b % 2, :, :, :].rearrange("q p h r -> q (p h) r")
                        nc.vector.tensor_copy(sums[:, bass.ds(h, 1), 0:DK], ps_m[:, 0:DK].unsqueeze(1)).then_inc(g_o_read, 1)
                        nc.vector.tensor_copy(sums[:, bass.ds(h, 1), DK:DK + 1], g_sum.unsqueeze(1)).then_inc(g_o_read, 1)
                    ve.wait_ge(g_o_read, 2 * H * (b + 1))
                    normalise(B + b)
                    tail(B + b)
                result(1)

        @block.tensor
        def _(pe):
            def put(task, dst):
                kind, b, what, c = task
                n = CHUNKS * b + c
                if what == "bias":
                    pe.wait_ge(up_b_ready, 1)
                    for j in range(HB):
                        ins = nc.tensor.matmul(dst[:, j:j + 1], up_b[:, 128 * j:128 * j + 128], ident[0:1, 0:1],
                                               start=True, stop=True)
                    ins.then_inc(up_bps, 1)
                elif what == "down":
                    pe.wait_ge(down_ready, 1)
                    for j in range(HB):
                        ins = nc.tensor.transpose(dst[:, 128 * j:128 * j + 128], down_y[:, 0, 128 * j:128 * j + 128], ident[:])
                    ins.then_inc(dn_tps, 1)
                elif what == "turn":
                    pe.wait_ge(in_ctx[c], 16 * (b + 1))
                    for t in range(4):
                        ins = nc.tensor.transpose(dst[:, 128 * t:128 * t + 128], ctx_sb[:, 4 * c + t, :], ident[:])
                    ins.then_inc(ctxT_ps, 1)
                elif what == "k":
                    pe.wait_ge(ctxT_ready, n + 1)
                    pe.wait_ge(in_wk, 32)
                    nc.tensor.matmul(dst, wk_sb[:], ctxT[:, 512 * c:512 * c + 512], start=True, stop=True).then_inc(k_ps, 1)
                elif what == "v":
                    pe.wait_ge(ctxT_ready, n + 1)
                    pe.wait_ge(in_wv, 16)
                    for t in range(4):
                        key = 512 * c + 128 * t
                        ins = nc.tensor.matmul(dst[:, 128 * t:128 * t + 128], ctxT[:, key:key + 128], wv_sb[:],
                                               start=True, stop=True)
                    ins.then_inc(v_ps, 1)
                elif what == "turn_att":
                    pe.wait_ge(att_ready, b + 1)
                    nc.tensor.transpose(dst[:, 0:S], att[:], ident[:]).then_inc(tail_ps, 1)
                elif what == "project":
                    pe.wait_ge(in_tail, 64)
                    nc.tensor.matmul(dst[:, 0:D], attT[:], wo_sb[:], start=True, stop=True).then_inc(tail_ps, 1)
                elif what in ("turn_x1", "turn_x2"):
                    pe.wait_ge(t_xn_ready, 2 * b + 1 + (what == "turn_x2"))
                    nc.tensor.transpose(dst[:, 0:S], t_xn[:], ident[:]).then_inc(tail_ps, 1)
                elif what == "qkv":
                    nc.tensor.matmul(dst[:, 0:S], aq_sb[:], t_xnT[:], start=True, stop=True)
                    nc.tensor.matmul(dst[:, S:2 * S], ak_sb[:], t_xnT[:], start=True, stop=True)
                    nc.tensor.matmul(dst[:, 2 * S:2 * S + D], t_xnT[:], av_sb[:], start=True, stop=True).then_inc(tail_ps, 1)
                elif what == "scores":
                    nc.tensor.matmul(dst[:, 0:S], s_qT[:], s_kT[:], start=True, stop=True).then_inc(tail_ps, 1)
                elif what == "turn_p":
                    nc.tensor.transpose(dst[:, 0:S], s_p[:], ident[:]).then_inc(tail_ps, 1)
                elif what == "self_out":
                    nc.tensor.matmul(dst[:, 0:D], s_pT[:], s_v[:], start=True, stop=True).then_inc(tail_ps, 1)

            def put_misc(task):
                pe.wait_ge(*before[task])
                if task[0] == "tail" and task[2] != TAIL[0]:
                    pe.wait_ge(tail_sb, len(TAIL) * task[1] + TAIL.index(task[2]))
                put(task, MISC[bank[task]])

            def scores_by_query(ua):
                g, k = divmod(ua, STEPS)
                b, p = divmod(g, PAIRS)
                if k == 0:
                    pe.wait_ge(*k_loaded(b, p))
                    pe.wait_ge(q_in[b], 16 * SLOTS)
                if ua >= 2:
                    pe.wait_ge(a_max, ua - 1)
                h, c = divmod(k, CHUNKS)
                nc.tensor.matmul(ps_a[:, ua % 2, :], qstack[0:ROWS, b, p, S * h:S * h + S],
                                 kstack[0:ROWS, b % 2, p, 512 * c:512 * c + 512], start=True, stop=True).then_inc(a_ps, 1)

            def scores_by_key(u):
                g, k = divmod(u, STEPS)
                b, p = divmod(g, PAIRS)
                if k == 0:
                    pe.wait_ge(m_ready, g + 1)
                    if g == 0:
                        pe.wait_ge(ones_in, 16 * 2)
                if u >= 2:
                    pe.wait_ge(p_ready, u - 1)
                for e in range(2):
                    key = 128 * (2 * k + e)
                    ins = nc.tensor.matmul(ps_b[:, u % 2, 256 * e:256 * e + 256],
                                           kstack[0:ROWS + MROWS, b % 2, p, key:key + 128],
                                           qstack[0:ROWS + MROWS, b, p, :], start=True, stop=True)
                ins.then_inc(b_ps, 1)

            def outputs(u):
                g, k = divmod(u, STEPS)
                b, p = divmod(g, PAIRS)
                pe.wait_ge(p_ready, u + 1)
                if k == 0:
                    if p == 0:
                        pe.wait_ge(v_ready, CHUNKS * (b + 1))
                    if g == 0:
                        pe.wait_ge(o_clear, 2)
                    if g >= 2:
                        pe.wait_ge(osum_ready, g - 1)
                for e in range(2):
                    for h in range(2):
                        j = 2 * e + h
                        ins = nc.tensor.matmul(ps_o[32 * j:32 * j + DK + 1, g % 2, 0:S],
                                               vt[:, b % 2, 2 * k + e, 2 * p + h, :],
                                               probs[:, u % 4, 128 * j:128 * j + 128],
                                               start=(k == 0), stop=(k == STEPS - 1))
                ins.then_inc(pv_done, 1)

            def turn_outputs(g):
                pe.wait_ge(oT_ready, g + 1)
                if g + 2 < G:
                    pe.wait_ge(m_ready, g + 3)
                nc.tensor.transpose(ps_o[:, g % 2, 128:256], oT[:, g % 2, :], ident[:]).then_inc(o_ps, 1)

            def turn_max(g):
                pe.wait_ge(mparts_ready, g + 1)
                if g >= 2:
                    pe.wait_ge(oT_ready, g - 1)
                for h in range(2):
                    ins = nc.tensor.transpose(ps_o[ROWS:ROWS + MROWS, g % 2, 256 + 64 * h:320 + 64 * h].bitcast(BF16),
                                              mparts[:, g % 2, h, :], identb[:])
                ins.then_inc(m_ps, 1)

            def turn_xn(i):
                for b in range(*PHASES[i]):
                    pe.wait_ge(xn_ready, b + 1)
                    ins = nc.tensor.transpose(ps_m[:, S * b:S * b + S], xn[:, b, :], ident[:])
                ins.then_inc(xnT_ps, 1)

            def project_q(i):
                sl = slice(S * PHASES[i][0], S * PHASES[i][1])
                pe.wait_ge(xnT_ready, i + 1)
                nc.tensor.matmul(ps_o[:, 0, sl], wq_sb[:], xnT[:, sl], start=True, stop=True).then_inc(q_ps, 1)

            def keep_clock(n, dst=ps_b[:, 0, 0:64]):
                for i in range(n):
                    nc.tensor.transpose(dst.bitcast(BF16), identb[:], identb[:])

            pe.wait_ge(consts, 1)
            keep_clock(WARM)
            put(("prep", 0, "turn", 0), ps_b[:, 0, :])
            turn_xn(0)
            keep_clock(KEEP, ps_a[:, 1, 0:64])
            pe.wait_ge(in_wq, 16)
            project_q(0)
            put(("prep", 0, "k", 0), K_BANK[0])
            put(("prep", 0, "turn", 1), ps_b[:, 1, :])
            put(("prep", 0, "turn", 2), ps_b[:, 2, :])
            put(("prep", 0, "k", 1), K_BANK[1])
            pe.wait_ge(ctxT_ready, 1)
            put(("prep", 0, "turn", 3), ps_b[:, 0, :])
            put(("prep", 0, "k", 2), K_BANK[2])
            turn_xn(1)
            put(("prep", 0, "k", 3), K_BANK[3])
            project_q(1)
            for c in range(CHUNKS):
                if c == 1:
                    pe.wait_ge(ctxT_ready, CHUNKS)
                if c == 3:
                    pe.wait_ge(v_ready, 1)
                put(("prep", 0, "v", c), V_BANK[c])
            pe.wait_ge(k2_ready, CHUNKS)
            pe.wait_ge(v_ready, CHUNKS)
            keep_clock(2 * WARM)
            for ua in range((AHEAD - 1) * STEPS):
                scores_by_query(ua)
                if ua in EARLY:
                    put_misc(("prep", 1) + EARLY[ua])
                else:
                    keep_clock(WARM // 3)
            for late in (STEPS, STEPS + 1):
                put_misc(("prep", 1) + EARLY[late])
            pe.wait_ge(o_clear, 2)
            turn_max(0)
            for g in range(G):
                for k in range(STEPS):
                    u = STEPS * g + k
                    scores_by_key(u)
                    for ua in ahead(g, k):
                        scores_by_query(ua)
                    if u >= LAG:
                        outputs(u - LAG)
                    if k == 5 and g + 1 < G:
                        turn_max(g + 1)
                    if k == 7 and g >= 1:
                        turn_outputs(g - 1)
                    if misc_task(g, k):
                        put_misc(misc_task(g, k))
            for u in range(STEPS * G - LAG, STEPS * G):
                outputs(u)
            pe.wait_ge(a_max, STEPS * G)
            keep_clock(KEEP, ps_a[:, 1, 0:64])
            turn_outputs(G - 1)
            keep_clock(KEEP, ps_a[:, 1, 0:64])
            def tail(b):
                for what in TAIL:
                    put_misc(("tail", b, what, 0))

            def up(turn, i, j):
                b0, b1 = FFN_PHASES[i]
                pe.wait_ge(tail_sb, len(TAIL) * (B * turn + b1))
                if (turn, i) == (0, 0):
                    pe.wait_ge(*((p_ready, STEPS * G), (p_ready, STEPS * G), second_free, (a_max, STEPS * G))[j])
                nc.tensor.matmul(up_bank(j)[:, S * b0:S * b1], up_y[:, STAGES % 2, 128 * j:128 * j + 128],
                                 f_xnT[:, S * b0:S * b1], start=True, stop=True).then_inc(up_ps, 1)

            def down(turn, b):
                i = int(b == B - 1)
                pe.wait_ge(w_dn_ready, 1)
                pe.wait_ge(gelu_ready, HB * (2 * turn + i + 1))
                if (turn, b) == (0, 0):
                    pe.wait_ge(low_read, 1)
                for j in range(HB):
                    ins = nc.tensor.matmul(DOWN_BANK[b][:, 0:D], f_h[:, j, S * b:S * b + S], w_dn[:, j, :],
                                           start=(j == 0), stop=(j == HB - 1))
                ins.then_inc(dn_ps, 1)

            def last_tail(turn):
                for what in TAIL:
                    put_misc(("tail", B * turn + B - 1, what, 0))
                    if turn == 0 and what not in ("turn_att", "project"):
                        keep_clock(KEEP, ps_a[:, 1, 0:64])
                    for j in {"turn_att": (0,), "project": (1, 2, 3)}.get(what, ()):
                        up(turn, 0, j)
                    if (turn, what) == (0, "turn_x1"):
                        pe.wait_ge(low_ready, 1)
                        pe.wait_ge(osum_ready, G)
                        nc.tensor.transpose(ps_o[0:1, 0, 0:128], mask_low[:], ident[:]).then_inc(low_ps, 1)
                for j in range(HB):
                    up(turn, 1, j)
                for b in range(B):
                    down(turn, b)

            last_tail(0)
            with masked(pe):
                for b in range(B):
                    for what, c in PREP:
                        put_misc(("prep", B + b, what, c))
                    pe.wait_ge(g_k_ready, CHUNKS * (b + 1))
                    pe.wait_ge(v_ready, CHUNKS * (B + b + 1))
                    with pe.Fori(0, H) as h:
                        n = h + H * b + 1
                        pe.wait_ge(g_qh_ready, n)
                        for c in range(CHUNKS):
                            ins = nc.tensor.matmul(g_bank(c), g_qh, g_kT[:, 512 * c:512 * c + 512], start=True, stop=True)
                        ins.then_inc(g_s_ps, 1)
                        pe.wait_ge(g_p_ready, n)
                        for t in range(KT):
                            ins = nc.tensor.transpose(g_bank(t // 4)[:, 128 * (t % 4):128 * (t % 4) + 128],
                                                      g_s[:, 128 * t:128 * t + 128], ident[:])
                        ins.then_inc(g_pT_ps, 1)
                        pe.wait_ge(g_pT_ready, n)
                        for t in range(KT):
                            ins = nc.tensor.matmul(ps_m[:, 0:DK], g_pT[:, 128 * t:128 * t + 128],
                                                   g_v[:, bass.ds(h * DK + D * t, DK)], start=(t == 0), stop=(t == KT - 1))
                        ins.then_inc(g_o_ps, 1)
                    pe.wait_ge(g_o_read, 2 * H * (b + 1))
                    if b < B - 1:
                        tail(B + b)
                last_tail(1)


def kernel(**inputs):
    import numpy as np
    import concourse.bacc as bacc
    from concourse.bass_utils import run_bass_kernel_spmd

    def arr(name):
        return np.asarray(inputs[name])

    def flat(a):
        return a.reshape(1, -1)

    arrays = {
        "x": arr("x"),
        "ctx": arr("ctx_1024"),
        "mask": arr("mask_Bx1xSxS2_if1"),
        "w_q": arr("L0_xattn_Wq"), "w_k": arr("L0_xattn_Wk"), "w_v": arr("L0_xattn_Wv"), "w_o": arr("L0_xattn_Wo"),
        "a_wqT": arr("L0_attn_wq").T, "a_wkT": arr("L0_attn_wk").T, "a_wvT": arr("L0_attn_wv").T,
        "w_exp": arr("L0_ffn_W_exp"), "b_exp": flat(arr("L0_ffn_b_exp")),
        "w_up": arr("L0_ffn_up_weights").reshape(len(arr("L0_ffn_up_weights")), -1),
        "up_bias": flat(arr("L0_ffn_up_bias")),
        "w_down": arr("L0_ffn_down_weights").reshape(len(arr("L0_ffn_down_weights")), -1),
        "w_conT": arr("L0_ffn_W_con").T,
        "bias_cols": np.stack([arr(n) for n in ("L0_xattn_bq", "L0_xattn_bk", "L0_xattn_bv", "L0_attn_bq", "L0_attn_bk")], axis=1),
        "bias_rows": np.concatenate([arr(n) for n in ("L0_xattn_bo", "L0_attn_bv", "L0_ffn_b_con", "L0_ffn_down_bias")]),
    }
    arrays = {n: np.ascontiguousarray(a) for n, a in arrays.items()}
    nc = bacc.Bacc("TRN2", target_bir_lowering=False, num_devices=1)
    aps = [nc.dram_tensor(f"in_{n}", a.shape, mybir.dt.from_np(a.dtype), kind="ExternalInput").ap() for n, a in arrays.items()]
    shape = arrays["x"].shape
    out = nc.dram_tensor("out_x", shape, F32, kind="ExternalOutput").ap()
    q_scratch = nc.dram_tensor("q_scratch", (128, 3, shape[0], 2 * shape[1]), BF16).ap()
    q_full = nc.dram_tensor("q_full", (128, shape[0] * shape[1]), F32).ap()
    row_scratch = nc.dram_tensor("row_scratch", arrays["b_exp"].shape, F32).ap()
    perceiver_block(nc, *aps, out, q_scratch, q_full, row_scratch)
    got = run_bass_kernel_spmd(nc, [{f"in_{n}": a for n, a in arrays.items()}], core_ids=[0])
    return got.results[0]["out_x"]
```
